# Optimizing a Trainium2 kernel written in Bass

```python
import numpy as np
import jax
import jax.numpy as jnp

def _softmax(x, axis=-1):
    return jax.nn.softmax(x, axis=axis)

def _gelu(x):
    return jax.nn.gelu(x, approximate=True)

def _silu(x):
    return jax.nn.silu(x)

def _sigmoid(x):
    return jax.nn.sigmoid(x)

def _layernorm(x, axis=-1, eps=1e-05):
    m = jnp.mean(x, axis=axis, keepdims=True)
    v = jnp.var(x, axis=axis, keepdims=True)
    return (x - m) / jnp.sqrt(v + eps)

def _scatter_add(tgt, idx, src, axis=0):
    return tgt.at[idx].add(src)

def _segment_sum(src, seg, n):
    return jax.ops.segment_sum(src, seg, n)
kernel_name = 'mk_cond_seq_d2_seqx_r2_7add1e'

def setup_inputs(seed: int=0):
    np.random.seed(seed)
    _w = jnp.asarray

    def _rec_inputs():
        import jax
        import jax.numpy as jnp
        _rk = jax.random.key(seed)
        x = -0.000125 + 0.9999 * jax.random.normal(jax.random.fold_in(_rk, 1), (8, 512, 512), jnp.float32)
        _lenS = 512 - jax.random.randint(jax.random.fold_in(_rk, 7), (8,), 0, max(1, 512 // 4) + 1, jnp.int32)
        _lenS2 = 512 - jax.random.randint(jax.random.fold_in(_rk, 8), (8,), 0, max(1, 512 // 4) + 1, jnp.int32)
        cond_1024 = 0.00782532 + 1.00527 * jax.random.normal(jax.random.fold_in(_rk, 11), (8, 512), jnp.float32)
        return (x, cond_1024)
    x, cond_1024 = _rec_inputs()

    def _L0_cond_setup():
        import jax, jax.numpy as jnp
        import numpy as np
        EPS_RMS = 1e-06
        EPS_Q = 1e-05

        def _weight_quant(w):
            scale = 1.0 / jnp.clip(jnp.mean(jnp.abs(w)), EPS_Q)
            wq = jnp.clip(jnp.round(w * scale), -1.0, 1.0) / scale
            return w + jax.lax.stop_gradient(wq - w)

        def _activation_quant(x):
            scale = 127.0 / jnp.clip(jnp.max(jnp.abs(x), axis=-1, keepdims=True), EPS_Q)
            xq = jnp.clip(jnp.round(x * scale), -128.0, 127.0) / scale
            return x + jax.lax.stop_gradient(xq - x)

        def _rmsnorm(x, weight):
            inv = jax.lax.rsqrt(jnp.mean(x * x, axis=-1, keepdims=True) + EPS_RMS)
            return x * inv * weight
        key = jax.random.key(seed)
        k1, k2, k3 = jax.random.split(key, 3)
        B, S, D, CD = (8, 2048, 512, 512)
        x = jax.random.normal(k1, (B, S, D), dtype=jnp.float32)
        c = jax.random.normal(k2, (B, CD), dtype=jnp.float32)
        w_proj = jax.random.normal(k3, (2 * D, CD), dtype=jnp.float32) * 0.02
        b_proj = jnp.zeros((2 * D,), dtype=jnp.float32)
        rms_weight = jnp.ones((D,), dtype=jnp.float32)
        return {'x': x, 'c': c, 'w_proj': w_proj, 'b_proj': b_proj, 'rms_weight': rms_weight}
    _L0_cond_all = _L0_cond_setup()
    _L0_cond_in = {k: v for k, v in _L0_cond_all.items() if k in ('w_proj', 'b_proj', 'rms_weight')}
    del _L0_cond_all

    def _L1_cond_setup():
        import jax, jax.numpy as jnp
        import numpy as np
        D_MODEL = 512
        N_HEADS = 16
        HEAD_DIM = D_MODEL // N_HEADS
        D_FF = 2048
        EPS = 1e-05
        THETA = 10000.0
        B, S = (2, 1024)

        def _rope_cache(seq_len, head_dim, theta=THETA):
            inv_freq = 1.0 / theta ** (jnp.arange(0, head_dim, 2, dtype=jnp.float32) / head_dim)
            t = jnp.arange(seq_len, dtype=jnp.float32)
            freqs = jnp.einsum('i,j->ij', t, inv_freq)
            emb = jnp.concatenate([freqs, freqs], axis=-1)
            return (jnp.cos(emb), jnp.sin(emb))

        def _rotate_half(x):
            x1, x2 = jnp.split(x, 2, axis=-1)
            return jnp.concatenate([-x2, x1], axis=-1)

        def _ada_rmsnorm(x, time_emb, weight, w1, b1, w2, b2):
            h = jax.nn.silu(time_emb @ w1 + b1)
            scale, shift = jnp.split(h @ w2 + b2, 2, axis=-1)
            norm = x * jax.lax.rsqrt(jnp.mean(x * x, axis=-1, keepdims=True) + EPS)
            return norm * weight * (1.0 + scale[:, None, :]) + shift[:, None, :]
        key = jax.random.key(seed)
        ks = jax.random.split(key, 24)
        rn = lambda k, shp: jax.random.normal(k, shp, dtype=jnp.float32) * 0.02
        return {'x': jax.random.normal(ks[0], (B, S, D_MODEL), dtype=jnp.float32), 'time_emb': jax.random.normal(ks[1], (B, D_MODEL), dtype=jnp.float32), 'w_norm1': jnp.ones((D_MODEL,), jnp.float32), 't1_w1': rn(ks[2], (D_MODEL, D_MODEL)), 't1_b1': jnp.zeros((D_MODEL,), jnp.float32), 't1_w2': rn(ks[3], (D_MODEL, 2 * D_MODEL)), 't1_b2': jnp.zeros((2 * D_MODEL,), jnp.float32), 'w_norm2': jnp.ones((D_MODEL,), jnp.float32), 't2_w1': rn(ks[4], (D_MODEL, D_MODEL)), 't2_b1': jnp.zeros((D_MODEL,), jnp.float32), 't2_w2': rn(ks[5], (D_MODEL, 2 * D_MODEL)), 't2_b2': jnp.zeros((2 * D_MODEL,), jnp.float32), 'wq': rn(ks[6], (D_MODEL, D_MODEL)), 'bq': jnp.zeros((D_MODEL,), jnp.float32), 'wk': rn(ks[7], (D_MODEL, D_MODEL)), 'bk': jnp.zeros((D_MODEL,), jnp.float32), 'wv': rn(ks[8], (D_MODEL, D_MODEL)), 'bv': jnp.zeros((D_MODEL,), jnp.float32), 'wo': rn(ks[9], (D_MODEL, D_MODEL)), 'bo': jnp.zeros((D_MODEL,), jnp.float32), 'w_gate': rn(ks[10], (D_MODEL, D_FF)), 'w_up': rn(ks[11], (D_MODEL, D_FF)), 'w_down': rn(ks[12], (D_FF, D_MODEL))}
    _L1_cond_all = _L1_cond_setup()
    _L1_cond_in = {k: v for k, v in _L1_cond_all.items() if k in ('w_norm1', 't1_w1', 't1_b1', 't1_w2', 't1_b2', 'w_norm2', 't2_w1', 't2_b1', 't2_w2', 't2_b2', 'wq', 'bq', 'wk', 'bk', 'wv', 'bv', 'wo', 'bo', 'w_gate', 'w_up', 'w_down')}
    del _L1_cond_all
    return {'x': x, 'cond_1024': cond_1024, 'L0_cond_w_proj': _L0_cond_in['w_proj'], 'L0_cond_b_proj': _L0_cond_in['b_proj'], 'L0_cond_rms_weight': _L0_cond_in['rms_weight'], 'L1_cond_w_norm1': _L1_cond_in['w_norm1'], 'L1_cond_t1_w1': _L1_cond_in['t1_w1'], 'L1_cond_t1_b1': _L1_cond_in['t1_b1'], 'L1_cond_t1_w2': _L1_cond_in['t1_w2'], 'L1_cond_t1_b2': _L1_cond_in['t1_b2'], 'L1_cond_w_norm2': _L1_cond_in['w_norm2'], 'L1_cond_t2_w1': _L1_cond_in['t2_w1'], 'L1_cond_t2_b1': _L1_cond_in['t2_b1'], 'L1_cond_t2_w2': _L1_cond_in['t2_w2'], 'L1_cond_t2_b2': _L1_cond_in['t2_b2'], 'L1_cond_wq': _L1_cond_in['wq'], 'L1_cond_bq': _L1_cond_in['bq'], 'L1_cond_wk': _L1_cond_in['wk'], 'L1_cond_bk': _L1_cond_in['bk'], 'L1_cond_wv': _L1_cond_in['wv'], 'L1_cond_bv': _L1_cond_in['bv'], 'L1_cond_wo': _L1_cond_in['wo'], 'L1_cond_bo': _L1_cond_in['bo'], 'L1_cond_w_gate': _L1_cond_in['w_gate'], 'L1_cond_w_up': _L1_cond_in['w_up'], 'L1_cond_w_down': _L1_cond_in['w_down']}

def reference(x, cond_1024, L0_cond_w_proj, L0_cond_b_proj, L0_cond_rms_weight, L1_cond_w_norm1, L1_cond_t1_w1, L1_cond_t1_b1, L1_cond_t1_w2, L1_cond_t1_b2, L1_cond_w_norm2, L1_cond_t2_w1, L1_cond_t2_b1, L1_cond_t2_w2, L1_cond_t2_b2, L1_cond_wq, L1_cond_bq, L1_cond_wk, L1_cond_bk, L1_cond_wv, L1_cond_bv, L1_cond_wo, L1_cond_bo, L1_cond_w_gate, L1_cond_w_up, L1_cond_w_down):
    import jax
    import jax.numpy as jnp

    def _L0_cond_ref(x, c, w_proj, b_proj, rms_weight):
        import jax, jax.numpy as jnp
        import numpy as np
        EPS_RMS = 1e-06
        EPS_Q = 1e-05

        def _weight_quant(w):
            scale = 1.0 / jnp.clip(jnp.mean(jnp.abs(w)), EPS_Q)
            wq = jnp.clip(jnp.round(w * scale), -1.0, 1.0) / scale
            return w + jax.lax.stop_gradient(wq - w)

        def _activation_quant(x):
            scale = 127.0 / jnp.clip(jnp.max(jnp.abs(x), axis=-1, keepdims=True), EPS_Q)
            xq = jnp.clip(jnp.round(x * scale), -128.0, 127.0) / scale
            return x + jax.lax.stop_gradient(xq - x)

        def _rmsnorm(x, weight):
            inv = jax.lax.rsqrt(jnp.mean(x * x, axis=-1, keepdims=True) + EPS_RMS)
            return x * inv * weight
        if c.ndim == 2:
            c = c[:, None, :]
        cq = _activation_quant(c)
        wq = _weight_quant(w_proj)
        emb = jnp.einsum('btc,dc->btd', cq, wq) + b_proj
        scale, shift = jnp.split(emb, 2, axis=-1)
        xn = _rmsnorm(x, rms_weight)
        return xn * (1.0 + scale) + shift

    def _L1_cond_ref(x, time_emb, w_norm1, t1_w1, t1_b1, t1_w2, t1_b2, w_norm2, t2_w1, t2_b1, t2_w2, t2_b2, wq, bq, wk, bk, wv, bv, wo, bo, w_gate, w_up, w_down):
        import jax, jax.numpy as jnp
        import numpy as np
        D_MODEL = 512
        N_HEADS = 16
        HEAD_DIM = D_MODEL // N_HEADS
        D_FF = 2048
        EPS = 1e-05
        THETA = 10000.0
        B, S = (2, 1024)

        def _rope_cache(seq_len, head_dim, theta=THETA):
            inv_freq = 1.0 / theta ** (jnp.arange(0, head_dim, 2, dtype=jnp.float32) / head_dim)
            t = jnp.arange(seq_len, dtype=jnp.float32)
            freqs = jnp.einsum('i,j->ij', t, inv_freq)
            emb = jnp.concatenate([freqs, freqs], axis=-1)
            return (jnp.cos(emb), jnp.sin(emb))

        def _rotate_half(x):
            x1, x2 = jnp.split(x, 2, axis=-1)
            return jnp.concatenate([-x2, x1], axis=-1)

        def _ada_rmsnorm(x, time_emb, weight, w1, b1, w2, b2):
            h = jax.nn.silu(time_emb @ w1 + b1)
            scale, shift = jnp.split(h @ w2 + b2, 2, axis=-1)
            norm = x * jax.lax.rsqrt(jnp.mean(x * x, axis=-1, keepdims=True) + EPS)
            return norm * weight * (1.0 + scale[:, None, :]) + shift[:, None, :]
        b, s, _ = x.shape
        cos, sin = _rope_cache(s, HEAD_DIM)
        nx = _ada_rmsnorm(x, time_emb, w_norm1, t1_w1, t1_b1, t1_w2, t1_b2)
        q = (nx @ wq + bq).reshape(b, s, N_HEADS, HEAD_DIM)
        k = (nx @ wk + bk).reshape(b, s, N_HEADS, HEAD_DIM)
        v = (nx @ wv + bv).reshape(b, s, N_HEADS, HEAD_DIM)
        c = cos[:, None, :]
        si = sin[:, None, :]
        q = q * c + _rotate_half(q) * si
        k = k * c + _rotate_half(k) * si
        scores = jnp.einsum('bshd,bthd->bhst', q, k) / jnp.sqrt(jnp.float32(HEAD_DIM))
        probs = jax.nn.softmax(scores, axis=-1)
        attn = jnp.einsum('bhst,bthd->bshd', probs, v).reshape(b, s, D_MODEL)
        x = x + attn @ wo + bo
        nx = _ada_rmsnorm(x, time_emb, w_norm2, t2_w1, t2_b1, t2_w2, t2_b2)
        gate = jax.nn.gelu(nx @ w_gate, approximate=False)
        ff = gate * (nx @ w_up) @ w_down
        return x + ff
    x = _L0_cond_ref(x, cond_1024, L0_cond_w_proj, L0_cond_b_proj, L0_cond_rms_weight)
    x = _L1_cond_ref(x, cond_1024, L1_cond_w_norm1, L1_cond_t1_w1, L1_cond_t1_b1, L1_cond_t1_w2, L1_cond_t1_b2, L1_cond_w_norm2, L1_cond_t2_w1, L1_cond_t2_b1, L1_cond_t2_w2, L1_cond_t2_b2, L1_cond_wq, L1_cond_bq, L1_cond_wk, L1_cond_bk, L1_cond_wv, L1_cond_bv, L1_cond_wo, L1_cond_bo, L1_cond_w_gate, L1_cond_w_up, L1_cond_w_down)
    return x

_drawn_inputs = setup_inputs


def setup_inputs(seed=0):
    import zlib

    import numpy as np

    out = dict(_drawn_inputs(seed))
    spreads = {'L0_cond_b_proj': (0.0, 0.1),
     'L0_cond_rms_weight': (1.0, 0.2),
     'L1_cond_w_norm1': (1.0, 0.6),
     'L1_cond_t1_b1': (0.0, 0.8),
     'L1_cond_t1_b2': (0.0, 0.437),
     'L1_cond_w_norm2': (1.0, 0.2),
     'L1_cond_t2_b1': (0.0, 0.8),
     'L1_cond_t2_b2': (0.0, 0.397),
     'L1_cond_bq': (0.0, 0.8),
     'L1_cond_bk': (0.0, 0.8),
     'L1_cond_bv': (0.0, 0.1),
     'L1_cond_bo': (0.0, 0.1)}
    factors = {'L1_cond_t1_w1': 2.672, 'L1_cond_t2_w1': 2.724, 'L1_cond_wq': 8.0, 'L1_cond_wk': 8.0}
    for name, (base, spread) in spreads.items():
        noise = np.random.default_rng([zlib.crc32(name.encode()), seed]).standard_normal(out[name].shape)
        drawn = base * np.exp(spread * noise) if base else spread * noise
        out[name] = jnp.asarray(drawn.astype(out[name].dtype))
    for name, factor in factors.items():
        out[name] = (out[name] * factor).astype(out[name].dtype)
    return out
```

```python
from contextlib import ExitStack

import concourse.bass as bass
from concourse import mybir

ALU = mybir.AluOpType
ACT = mybir.ActivationFunctionType
F32 = mybir.dt.float32
F16 = mybir.dt.float16
AX_X = mybir.AxisListType.X

P = 128
B, S, D = 8, 512, 512
H, HD = 16, 32
F = 2048
TT = S // P
KT = D // P
FT = F // P
FH = FT // 2
W_SCALE = 256.0
SQRT_D = float(D) ** 0.5
UNSCALE = 1.0 / W_SCALE
LN_SCALE = 8 * 0.6931471805599453
RING = 3
WRING = 2
VW = 2 * HD + 1


def bank_turns():
    steps = [("n1", k) for k in range(KT)]
    for t in range(TT):
        steps += [("qkv", t, m) for m in "qkv"]
        if t:
            steps += [("st", t - 1, m, g) for m in "qk" for g in range(2)]
    steps += [("st", TT - 1, m, g) for m in "qk" for g in range(2)]
    steps += [("mt",)] + [("ot", k) for k in range(KT)] + [("wo", t) for t in range(TT)]
    steps += [("n2", k) for k in range(KT)]
    for half in range(2):
        for f in range(half * FH, half * FH + FH):
            steps += [("g", f), ("u", f)]
        steps += [("dn", half, t) for t in range(TT)]
    return {s: n for n, s in enumerate(steps)}


TURN = bank_turns()
PER_BANK = [len(range(k, len(TURN), RING)) for k in range(RING)]


def turn(it, *step):
    n = TURN[step]
    return n % RING, it * PER_BANK[n % RING] + n // RING + 1


def prepare(nc, ctx, w, res, scratch):
    def sb(name, shape, dt=F32):
        return ctx.enter_context(nc.sbuf_tensor(name, shape, dt))

    def sem(name):
        return ctx.enter_context(nc.semaphore(name))

    stage = sb("p_stage", [P, 3, 2048])
    hi_out = sb("p_hi", [P, 2, 2048], F16)
    lo_out = sb("p_lo", [P, 2, 2048], F16)
    cond = sb("p_cond", [B, D])
    cond_t = sb("p_cond_t", [P, KT, B])
    wp = sb("p_wp", [P, 8, 512])
    tern = sb("p_tern", [P, 8, 512], F16)
    tern_t = sb("p_tern_t", [P, KT, 1024], F16)
    pick = sb("p_pick", [P, H], F16)
    absum = sb("p_absum", [P, 1])
    mean = sb("p_mean", [P, 1])
    wscale = sb("p_wscale", [P, 1])
    cmax = sb("p_cmax", [B, 1])
    cinv = sb("p_cinv", [B, 1])
    cfac = sb("p_cfac", [B, 1])
    cint = sb("p_cint", [B, D])
    cint16 = sb("p_cint16", [B, D], F16)
    cint_t = sb("p_cint_t", [P, KT, B], F16)
    bproj = sb("p_bproj", [B, 1024])
    rmsw = sb("p_rmsw", [B, D])
    emb = sb("p_emb", [B, 1024])
    ones = sb("p_ones", [P, P])
    w1 = sb("p_w1", [P, KT, 512])
    w2 = sb("p_w2", [P, KT, 1024])
    vecs = sb("p_vecs", [P, 2, 4 * KT])
    b1, b2, wn = vecs[:, :, 0:KT], vecs[:, :, KT:3 * KT], vecs[:, :, 3 * KT:4 * KT]
    z = sb("p_z", [P, KT, B])
    ez = sb("p_ez", [P, KT, B])
    y = sb("p_y", [P, 8, B])
    mods = sb("p_mods", [P, B, 2, 2, KT])
    bias2 = tern_t[0:64, :, :].rearrange("p k n -> p (k n)").bitcast(F32).rearrange("p (m n) -> p m n", m=4)

    ps_t = ctx.enter_context(nc.psum_tensor("p_ps_t", [P, 2, 1024], F16))
    ps_e = ctx.enter_context(nc.psum_tensor("p_ps_e", [P, 2, 512], F32))
    ps_s = ctx.enter_context(nc.psum_tensor("p_ps_s", [P, 512], F32))
    ps_m = ctx.enter_context(nc.psum_tensor("p_ps_m", [P, 512], F32))

    staged = [sem(f"p_staged{i}") for i in range(3)]
    hi_done, lo_done = sem("p_hi_done"), sem("p_lo_done")
    kept = [sem("p_kept0"), sem("p_kept1")]
    small, wp_in, w12_in = sem("p_small"), sem("p_wp_in"), sem("p_w12_in")
    consts_in = sem("p_consts_in")
    v = sem("p_vector_step")
    abs_done, tr_done, tr_free = sem("p_abs_done"), sem("p_tr_done"), sem("p_tr_free")
    sum_done, emb_done, emb_out = sem("p_sum_done"), sem("p_emb_done"), sem("p_emb_out")
    ones_set = sem("p_ones_set")
    mlp1, mlp2, sil = sem("p_mlp1"), sem("p_mlp2"), sem("p_silu")
    z_ready, h_ready, y_used = sem("p_z_ready"), sem("p_h_ready"), sem("p_y_used")
    mods_ready, mods_out = sem("p_mods_ready"), sem("p_mods_out")
    bias_in, bias_hi = sem("p_bias_in"), sem("p_bias_hi")

    units = []
    for m, name in enumerate(["wq", "wk", "wv", "wo"]):
        units.append((w[name].rearrange("(k p) n -> p k n", p=P), ("qkvo", m)))
    for g, name in enumerate(["w_gate", "w_up"]):
        for k in range(KT):
            units.append((w[name][k * P:(k + 1) * P, :], ("gu", g, k)))
    for c in range(4):
        units.append((w["w_down"][c * 512:(c + 1) * 512, :].rearrange("(f p) n -> p f n", p=P), ("dn", c)))
    order = units[:4] + units[4:]
    n_gu = [n for n, u in enumerate(order) if u[1][0] == "gu"]

    def place(n):
        kind = order[n][1]
        if kind[0] == "qkvo":
            return [res["wqkvo"][:, kind[1], i, :, :] for i in range(2)]
        if kind[0] == "dn":
            return [res["wdn"][:, i, 4 * kind[1]:4 * kind[1] + 4, :] for i in range(2)]
        j = n_gu.index(n) % 2
        return [x[:, j, :] for x in (hi_out, lo_out)]

    def staging(n):
        ap = stage[:, n % 3, :]
        if order[n][1][0] != "gu":
            ap = ap.rearrange("p (k n) -> p k n", k=4)
        return ap

    def put_copy(sp, n):
        _, g, k = order[n][1]
        j = n_gu.index(n)
        sp.wait_ge(lo_done, n + 1)
        for i, src in enumerate((hi_out, lo_out)):
            dst = scratch["gu"][:, :, g, i, k, :].rearrange("f p n -> p f n")
            sp.dma_start(dst, src[:, j % 2, :].rearrange("p (f n) -> p f n", f=FT)).then_inc(kept[j % 2], 16)

    block = ctx.enter_context(nc.Block())

    @block.sync
    def _(sp):
        sp.dma_start(res["ident16"][:, :], w["ident16"]).then_inc(consts_in, 16)
        sp.dma_start(res["ident32"][:, :], w["ident32"]).then_inc(consts_in, 16)
        sp.dma_start(res["rope"][:, :, :, :], w["rope"].rearrange("(t p) c j -> p t c j", p=P)).then_inc(consts_in, 16)
        sp.dma_start(pick[96:128, :], w["pick"]).then_inc(consts_in, 16)
        for n, (src, _) in enumerate(order):
            if n >= 3:
                sp.wait_ge(lo_done, n - 2)
            sp.dma_start(staging(n), src).then_inc(staged[n % 3], 16)
            if n >= 2 and n - 2 in n_gu:
                put_copy(sp, n - 2)
        for n in range(len(order) - 2, len(order)):
            if n in n_gu:
                put_copy(sp, n)
        sp.wait_ge(mods_ready, 4)
        sp.dma_start(scratch["mods"].rearrange("b p c -> p b c"),
                     mods[:, :, :, :, :].rearrange("p b s a k -> p b (s a k)")).then_inc(mods_out, 16)
        sp.wait_ge(mods_out, 16)
        sp.wait_ge(kept[0], 16 * len(n_gu))
        sp.wait_ge(kept[1], 16 * len(n_gu))

    @block.gpsimd
    def _(pool):
        nc.gpsimd.memset(ones[:, :], 1.0).then_inc(ones_set, 1)
        pool.dma_start(wp[:, :, :], w["w_proj"].rearrange("(r p) c -> p r c", p=P)).then_inc(wp_in, 16)
        pool.dma_start(cond[:, :], w["cond"]).then_inc(small, 16)
        pool.dma_start(bproj[:, :], w["b_proj"].rearrange("(o n) -> o n", o=1).to_broadcast([B, 1024])).then_inc(small, 16)
        pool.dma_start(rmsw[:, :], w["rms_weight"].rearrange("(o n) -> o n", o=1).to_broadcast([B, D])).then_inc(small, 16)
        pool.dma_start(cond_t[:, :, :], w["cond_t"]).then_inc(small, 16)
        pool.dma_start(vecs[:, :, :], w["vecs"]).then_inc(small, 16)
        for m, name in enumerate(["bq", "bk", "bv", "bo"]):
            row = w[name].rearrange("(o n) -> o n", o=1)
            pool.dma_start(bias2[0:1, m, :], row).then_inc(bias_in, 16)
            pool.dma_start(bias2[32:33, m, :], row).then_inc(bias_in, 16)
        for i in range(2):
            if i:
                pool.wait_ge(mlp2, 1)
            pool.dma_start(w1[:, :, :], w[f"t{i+1}_w1"].rearrange("(k p) n -> p k n", p=P)).then_inc(w12_in, 16)
            pool.dma_start(w2[:, :, :], w[f"t{i+1}_w2"].rearrange("(k p) n -> p k n", p=P)).then_inc(w12_in, 16)
        pool.wait_ge(v, 17)
        pool.dma_start(scratch["rows"], emb[:, :]).then_inc(emb_out, 16)
        pool.wait_ge(emb_out, 16)

    @block.scalar
    def _(act):
        act.wait_ge(wp_in, 16)
        nc.scalar.activation(tern[:, :, :], wp[:, :, :], ACT.Abs, accum_out=absum[:, :]).then_inc(abs_done, 1)
        for n in range(len(order)):
            act.wait_ge(staged[n % 3], 16 * (n // 3 + 1))
            if n in n_gu and n_gu.index(n) >= 2:
                j = n_gu.index(n)
                act.wait_ge(kept[j % 2], 32 * (j // 2))
            nc.scalar.activation(place(n)[0], staging(n), ACT.Copy, scale=W_SCALE).then_inc(hi_done, 1)
            if n in (3, 9):
                i = int(n == 9)
                act.wait_ge(z_ready, i + 1)
                nc.scalar.activation(ez[:, :, :], z[:, :, :], ACT.Exp, scale=-1.0).then_inc(sil, 1)

    @block.tensor
    def _(pe):
        pe.wait_ge(consts_in, 64)
        pe.wait_ge(ones_set, 1)
        pe.wait_ge(abs_done, 1)
        nc.tensor.matmul(ps_s[:, 0:1], ones[:, :], absum[:, :], start=True, stop=True).then_inc(sum_done, 1)
        for i in range(2):
            pe.wait_ge(small, 16 * 5)
            pe.wait_ge(w12_in, 32 * (i + 1))
            if i:
                pe.wait_ge(y_used, 1)
            for m in range(KT):
                for k in range(KT):
                    mm = nc.tensor.matmul(ps_m[:, m * B:(m + 1) * B], w1[:, k, m * P:(m + 1) * P], cond_t[:, k, :],
                                          start=(k == 0), stop=(k == KT - 1))
            mm.then_inc(mlp1, 1)
            pe.wait_ge(h_ready, i + 1)
            for m in range(8):
                for k in range(KT):
                    mm = nc.tensor.matmul(ps_m[:, 64 + m * B:64 + (m + 1) * B], w2[:, k, m * P:(m + 1) * P], z[:, k, :],
                                          start=(k == 0), stop=(k == KT - 1))
            mm.then_inc(mlp2, 1)
        pe.wait_ge(v, 8)
        for k in range(KT):
            if k >= 2:
                pe.wait_ge(tr_free, k - 1)
            for r in range(8):
                mm = nc.tensor.transpose(ps_t[:, k % 2, r * P:(r + 1) * P], tern[:, r, k * P:(k + 1) * P], res["ident16"][:, :])
            mm.then_inc(tr_done, 1)
        pe.wait_ge(v, 12)
        pe.wait_ge(tr_free, 3)
        for k in range(KT):
            mm = nc.tensor.transpose(ps_t[:, 0, k * B:(k + 1) * B], cint16[:, k * P:(k + 1) * P], res["ident16"][0:B, 0:B])
        mm.then_inc(tr_done, 1)
        pe.wait_ge(tr_free, 5)
        for c in range(2):
            for k in range(KT):
                mm = nc.tensor.matmul(ps_e[0:B, c, :], cint_t[:, k, :], tern_t[:, k, c * 512:(c + 1) * 512],
                                      start=(k == 0), stop=(k == KT - 1))
        mm.then_inc(emb_done, 1)

    @block.vector
    def _(dve):
        n_step = [0]

        def then(ins):
            n_step[0] += 1
            ins.then_inc(v, 1)
            dve.wait_ge(v, n_step[0])

        def split_lo(n):
            dve.wait_ge(hi_done, n + 1)
            hi, lo = place(n)
            nc.vector.scalar_tensor_tensor(out=lo, in0=staging(n), scalar=W_SCALE, in1=hi,
                                           op0=ALU.mult, op1=ALU.subtract).then_inc(lo_done, 1)

        nc.vector.memset(res["brow"][:, :, :], 0.0)
        nc.vector.memset(res["bones"][:, :, :], 0.0)
        then(nc.vector.memset(res["v"][:, :, :, 2 * HD:VW], 1.0))
        for r in (0, 32):
            nc.vector.memset(res["bones"][r:r + 1, 0, :], 1.0)
            nc.vector.memset(res["bones"][r:r + 1, 1, :], W_SCALE)
        dve.wait_ge(consts_in, 64)
        then(nc.vector.tensor_copy(res["kT"][96:128, :, :], pick[96:128, :].rearrange("p (h o) -> p h o", o=1).to_broadcast([32, H, S])))
        dve.wait_ge(bias_in, 16 * 8)
        then(nc.vector.tensor_scalar(bias2[0:1, :, :], bias2[0:1, :, :], W_SCALE, None, ALU.mult))
        nc.vector.tensor_copy(res["brow"][0:1, :, :], bias2[0:1, :, :]).then_inc(bias_hi, 1)
        then(nc.vector.tensor_scalar(res["brow"][32:33, :, :], bias2[32:33, :, :], W_SCALE, None, ALU.mult))
        nc.vector.scalar_tensor_tensor(out=res["brow"][32:33, :, :], in0=bias2[32:33, :, :], scalar=W_SCALE,
                                       in1=res["brow"][32:33, :, :], op0=ALU.mult, op1=ALU.subtract)
        magic = 12582912.0
        dve.wait_ge(sum_done, 1)
        then(nc.vector.tensor_scalar(mean[:, :], ps_s[:, 0:1], 1.0 / (1024 * 512), 1e-5, ALU.mult, ALU.max))
        then(nc.vector.reciprocal(wscale[:, :], mean[:, :]))
        then(nc.vector.tensor_scalar(wp[:, :, :], wp[:, :, :], wscale[:, 0:1], magic, ALU.mult, ALU.add))
        for n in range(2):
            split_lo(n)
        then2 = nc.vector.tensor_scalar(wp[:, :, :], wp[:, :, :], -magic, -1.0, ALU.add, ALU.max)
        then2.then_inc(bias_hi, 1)
        dve.wait_ge(bias_hi, 2)
        then(nc.vector.tensor_scalar(tern[:, :, :], wp[:, :, :], 1.0, None, ALU.min))
        split_lo(2)
        dve.wait_ge(small, 16 * 5)
        then(nc.vector.tensor_reduce(cmax[:, :], cond[:, :], AX_X, ALU.max, apply_absolute_value=True))
        nc.vector.tensor_scalar(cmax[:, :], cmax[:, :], 1e-5, None, ALU.max).then_inc(bias_hi, 1)
        dve.wait_ge(bias_hi, 3)
        then(nc.vector.reciprocal(cinv[:, :], cmax[:, :]))
        nc.vector.tensor_scalar(cinv[:, :], cinv[:, :], 127.0, None, ALU.mult).then_inc(bias_hi, 1)
        dve.wait_ge(bias_hi, 4)
        then(nc.vector.tensor_scalar(cint[:, :], cond[:, :], cinv[:, 0:1], magic, ALU.mult, ALU.add))
        nc.vector.tensor_scalar(cint[:, :], cint[:, :], -magic, -128.0, ALU.add, ALU.max).then_inc(bias_hi, 1)
        dve.wait_ge(bias_hi, 5)
        then(nc.vector.tensor_scalar(cint16[:, :], cint[:, :], 127.0, None, ALU.min))
        then(nc.vector.tensor_scalar(cfac[:, :], cmax[:, :], 1.0 / 127.0, mean[0:B, 0:1], ALU.mult, ALU.mult))
        for i in range(2):
            dve.wait_ge(mlp1, i + 1)
            nc.vector.tensor_tensor(z[:, :, :], ps_m[:, 0:KT * B].rearrange("p (k b) -> p k b", b=B),
                                    b1[:, i, :].rearrange("p (k o) -> p k o", o=1).to_broadcast([P, KT, B]), ALU.add).then_inc(z_ready, 1)
            if i == 0:
                split_lo(3)
            else:
                split_lo(9)
            dve.wait_ge(sil, i + 1)
            nc.vector.tensor_scalar(ez[:, :, :], ez[:, :, :], 1.0, None, ALU.add).then_inc(mods_ready, 1)
            dve.wait_ge(mods_ready, 2 * i + 1)
            nc.vector.reciprocal(ez[:, :, :], ez[:, :, :]).then_inc(bias_hi, 1)
            dve.wait_ge(bias_hi, 6 + i)
            dve.wait_ge(z_ready, i + 1)
            nc.vector.tensor_tensor(z[:, :, :], z[:, :, :], ez[:, :, :], ALU.mult).then_inc(h_ready, 1)
            if i == 0:
                for n in range(4, 7):
                    split_lo(n)
            dve.wait_ge(mlp2, i + 1)
            nc.vector.tensor_tensor(y[:, :, :], ps_m[:, 64:64 + 8 * B].rearrange("p (k b) -> p k b", b=B),
                                    b2[:, i, :].rearrange("p (k o) -> p k o", o=1).to_broadcast([P, 8, B]), ALU.add).then_inc(y_used, 1)
            dve.wait_ge(y_used, 2 * i + 1)
            nc.vector.tensor_scalar(y[:, 0:KT, :], y[:, 0:KT, :], 1.0, SQRT_D, ALU.add, ALU.mult).then_inc(y_used, 1)
            dve.wait_ge(y_used, 2 * i + 2)
            wnb = wn[:, i, :].rearrange("p (k o) -> p k o", o=1).to_broadcast([P, KT, B])
            nc.vector.tensor_tensor(mods[:, :, i, 0, :].rearrange("p b k -> p k b"), y[:, 0:KT, :], wnb, ALU.mult)
            nc.vector.tensor_copy(mods[:, :, i, 1, :].rearrange("p b k -> p k b"), y[:, KT:8, :]).then_inc(mods_ready, 1)
            if i == 0:
                for n in range(7, 9):
                    split_lo(n)
        for k in range(KT):
            dve.wait_ge(tr_done, k + 1)
            nc.vector.tensor_copy(tern_t[:, k, :], ps_t[:, k % 2, :]).then_inc(tr_free, 1)
        dve.wait_ge(tr_done, 5)
        nc.vector.tensor_copy(cint_t[:, :, :], ps_t[:, 0, 0:KT * B].rearrange("p (k b) -> p k b", b=B)).then_inc(tr_free, 1)
        for n in range(10, 13):
            split_lo(n)
        dve.wait_ge(emb_done, 1)
        for c in range(2):
            nc.vector.scalar_tensor_tensor(out=emb[:, c * 512:(c + 1) * 512], in0=ps_e[0:B, c, :], scalar=cfac[:, 0:1],
                                           in1=bproj[:, c * 512:(c + 1) * 512], op0=ALU.mult, op1=ALU.add).then_inc(v, 1)
        dve.wait_ge(v, 15)
        nc.vector.scalar_tensor_tensor(out=emb[:, 0:D], in0=emb[:, 0:D], scalar=1.0, in1=rmsw[:, :],
                                       op0=ALU.add, op1=ALU.mult).then_inc(v, 1)
        dve.wait_ge(v, 16)
        nc.vector.tensor_scalar(emb[:, 0:D], emb[:, 0:D], SQRT_D, None, ALU.mult).then_inc(v, 1)
        for n in range(13, len(order)):
            split_lo(n)
        for s in res["free"]:
            dve.sem_inc(s, 1)


def sequences(nc, ctx, w, res, scratch, out):
    def sb(name, shape, dt=F32):
        return ctx.enter_context(nc.sbuf_tensor(name, shape, dt))

    def sem(name):
        return ctx.enter_context(nc.semaphore(name))

    wq, wdn, ident16, ident32 = res["wqkvo"], res["wdn"], res["ident16"], res["ident32"]
    rope, kT, v, brow, bones = res["rope"], res["kT"], res["v"], res["brow"], res["bones"]
    bank_free, pair_free, pv_free, xin_free, stored = (
        res["bank_free"], res["pair_free"], res["pv_free"], res["xin_free"], res["stored"])

    xin = sb("xin", [P, TT, D])
    x1 = sb("x1", [P, TT, D])
    rows = sb("rows", [P, 2, D])
    mods = sb("mods", [P, 2, 2, KT])
    ssq = sb("ssq", [P, 3, TT])
    inv = sb("inv", [P, 3, TT])
    half = sb("half", [P, TT])
    eps_d = sb("eps_d", [P, 2, TT])
    nxT = sb("nxT", [P, 2, KT, S], F16)
    qT = sb("qT", [P, H, S], F16)
    wgu = sb("wgu", [P, WRING, 2, 2, KT, P], F16)
    acts = sb("acts", [P, 2, 512])
    hf = sb("hf", [P, 2, 512])
    hT = sb("hT", [P, 2, FH, S], F16)
    osb = sb("osb", [P, TT, H, HD])
    den = sb("den", [P, TT, H])
    rden = sb("rden", [P, TT, H])
    p32 = sb("p32", [P, 2, 2, S])
    front = sb("front", [P, 2, 2, TT * S], F16)
    mx = sb("mx", [P, H, TT])
    nmf = sb("nmf", [P, TT, H])
    nm = sb("nm", [P, TT, H, 2], F16)
    mrow = sb("mrow", [P, S], F16)
    junk = sb("junk", [P, D], F16)
    front_flat = front[:, :, :, :].rearrange("p a b n -> p (a b n)")
    rt = front_flat[:, 0:4096].bitcast(F32).rearrange("p (m i n) -> p m i n", m=2, i=2)
    stack = front_flat[:, 4096:4096 + 2 * H * 96].rearrange("p (m h c) -> p m h c", m=2, h=H)

    pair = [ctx.enter_context(nc.psum_tensor(f"pair{j}", [P, 2, 512], F32)) for j in range(2)]
    pvb = ctx.enter_context(nc.psum_tensor("pvb", [P, 512], F32))
    bank = [ctx.enter_context(nc.psum_tensor(f"bank{k}", [P, 512], F32)) for k in range(RING)]

    bank_filled = [sem(f"bank{k}_filled") for k in range(RING)]
    pair_filled = [sem(f"pair{j}_filled") for j in range(2)]
    pv_filled, pv_read = sem("pv_filled"), sem("pv_read")
    x_in, rows_in, mods_in = sem("x_in"), sem("rows_in"), sem("mods_in")
    wgu_in = [sem(f"wgu_in{i}") for i in range(WRING)]
    half_set = sem("half_set")
    sq = [sem(f"sq{i}") for i in range(3)]
    inv_pre, inv_ready = [sem(f"inv_pre{i}") for i in range(3)], [sem(f"inv_ready{i}") for i in range(3)]
    x1a, x1_ready, xn_ready = sem("x1a"), sem("x1_ready"), sem("xn_ready")
    nx_hi, nx_ready = sem("nx_hi"), sem("nx_ready")
    rope_a, rope_sum, rope_hi, rope_ready = sem("rope_a"), sem("rope_sum"), sem("rope_hi"), sem("rope_ready")
    v_hi = sem("v_hi")
    nm_step, nm_ready = sem("nm_step"), sem("nm_ready")
    mrow_in = sem("mrow_in")
    p_hi, p_ready = sem("p_hi"), sem("p_ready")
    o_copied, o_added, rden_ready, o_ready = sem("o_copied"), sem("o_added"), sem("rden_ready"), sem("o_ready")
    ot_hi = sem("ot_hi")
    h_hi, h_ready = sem("h_hi"), sem("h_ready")

    PARTS = [(0, 0), (0, 1), (1, 0)]
    INV_SQRT_HD = 1.0 / float(HD) ** 0.5

    block = ctx.enter_context(nc.Block())

    @block.sync
    def _(sp):
        for f in range(WRING):
            sp.dma_start(wgu[:, f, :, :, :, :], scratch["gu"][f]).then_inc(wgu_in[f], 16)
        with sp.Fori(0, B) as it:
            n, c = turn(it, "mt")
            sp.wait_ge(bank_free[n], c + 1)
            sp.dma_start(qT[96:128, :, :], mrow[96:128, :].rearrange("p (o s) -> p o s", o=1).to_broadcast([32, H, S])).then_inc(mrow_in, 16)
            for f in range(FT):
                n, c = turn(it, "u", f)
                sp.wait_ge(bank_filled[n], c)
                sp.dma_start(wgu[:, f % WRING, :, :, :, :], scratch["gu"][(f + WRING) % FT]).then_inc(wgu_in[f % WRING], 16)
            for t in range(TT):
                n, c = turn(it, "dn", 1, t)
                sp.wait_ge(bank_free[n], c + 1)
                sp.dma_start(out[it, t * P:(t + 1) * P, :], x1[:, t, :]).then_inc(stored, 16)
        sp.wait_ge(stored, 16 * TT * B + 1)
        for i in range(WRING):
            sp.wait_ge(wgu_in[i], 16 * (B * FT // WRING + 1))

    @block.gpsimd
    def _(pool):
        nc.gpsimd.memset(half[:, :], -0.5).then_inc(half_set, 1)
        nc.gpsimd.memset(eps_d[:, 0, :], 1e-6 * D).then_inc(half_set, 1)
        nc.gpsimd.memset(eps_d[:, 1, :], 1e-5 * D).then_inc(half_set, 1)
        pool.wait_ge(half_set, 3)
        with pool.Fori(0, B) as it:
            pool.wait_ge(xin_free, it + 1)
            pool.dma_start(xin[:, :, :], w["x"][it].rearrange("(t p) d -> p t d", p=P)).then_inc(x_in, 16)
            pool.dma_start(rows[:, :, :].rearrange("p c d -> p (c d)"), scratch["rows"][bass.ds(it, 1), :].to_broadcast([P, 2 * D])).then_inc(rows_in, 16)
            pool.dma_start(mods[:, :, :, :].rearrange("p s a k -> p (s a k)"), scratch["mods"][it]).then_inc(mods_in, 16)
            for i in range(3):
                pool.wait_ge(sq[i], it * TT + TT)
                nc.gpsimd.tensor_tensor(ssq[:, i, :], ssq[:, i, :], eps_d[:, min(i, 1), :], ALU.add).then_inc(inv_pre[i], 1)
                pool.wait_ge(inv_pre[i], it + 1)
                nc.gpsimd.tensor_tensor(inv[:, i, :], ssq[:, i, :], half[:, :], ALU.pow).then_inc(inv_ready[i], 1)

    @block.tensor
    def _(pe):
        def norm_transposes(it, which, ready):
            for k in range(KT):
                n, c = turn(it, which, k)
                pe.wait_ge(bank_free[n], c)
                for t in range(TT):
                    if k == 0:
                        pe.wait_ge(xn_ready, it * 2 * TT + ready + t + 1)
                    mm = nc.tensor.transpose(bank[n][:, t * P:(t + 1) * P], xin[:, t, k * P:(k + 1) * P], ident32[:, :])
                mm.then_inc(bank_filled[n], 1)

        def project(it, step, lhs, rhs, steps, bias=None, wait=None):
            n, c = turn(it, *step)
            pe.wait_ge(bank_free[n], c)
            if bias is not None:
                nc.tensor.matmul(bank[n][:, :], bones[:, bias[1], :], brow[:, bias[0], :], start=True, stop=False)
            for k in range(steps):
                if wait is not None:
                    wait(k)
                for a, b in PARTS:
                    mm = nc.tensor.matmul(bank[n][:, :], lhs(a, k), rhs(b, k), start=(bias is None and k == 0 and a + b == 0),
                                          stop=(k == steps - 1 and (a, b) == PARTS[-1]))
            mm.then_inc(bank_filled[n], 1)
            return mm

        def stack_transposes(it, t):
            for m, name in enumerate("qk"):
                pe.wait_ge(rope_ready, it * 2 * TT + 2 * t + m + 1)
                for g in range(2):
                    n, c = turn(it, "st", t, name, g)
                    pe.wait_ge(bank_free[n], c)
                    dst = bank[n][:, :].bitcast(F16)
                    for h in range(8):
                        mm = nc.tensor.transpose(dst[0:96, h * P:(h + 1) * P], stack[:, m, 8 * g + h, :], ident16[:, :])
                    mm.then_inc(bank_filled[n], 1)

        def probs_v(it, h):
            pe.wait_ge(p_ready, it * 2 * H + 2 * h + 2)
            pe.wait_ge(pv_free, it * H + h + 1)
            for s in range(TT):
                for k in range(TT):
                    for a in range(2):
                        mm = nc.tensor.matmul(pvb[:, s * VW:(s + 1) * VW], front[:, h % 2, a, k * S + s * P:k * S + (s + 1) * P],
                                              v[:, k, h, :], start=(k == 0 and a == 0), stop=(k == TT - 1 and a == 1))
            mm.then_inc(pv_filled, 1)

        with pe.Fori(0, B) as it:
            norm_transposes(it, "n1", 0)
            pe.wait_ge(nx_ready, it * 2 * KT + KT)
            for t in range(TT):
                for m, name in enumerate("qkv"):
                    project(it, ("qkv", t, name), lambda a, k: nxT[:, a, k, t * P:(t + 1) * P],
                            lambda b, k: wq[:, m, b, k, :], KT, bias=(m, 0))
                if t:
                    stack_transposes(it, t - 1)
            stack_transposes(it, TT - 1)
            for step in [("st", TT - 1, "q", 1), ("st", TT - 1, "k", 0), ("st", TT - 1, "k", 1)]:
                n, c = turn(it, *step)
                pe.wait_ge(bank_free[n], c + 1)
            for h in range(H):
                for j in range(2):
                    pe.wait_ge(pair_free[j], it * 2 * H + h + 1)
                    for i in range(2):
                        t = 2 * j + i
                        mm = nc.tensor.matmul(pair[j][:, i, :], qT[0:96, h, t * P:(t + 1) * P], kT[0:96, h, :], start=True, stop=True)
                    mm.then_inc(pair_filled[j], 1)
            pe.wait_ge(nm_ready, it + 1)
            n, c = turn(it, "mt")
            pe.wait_ge(bank_free[n], c)
            for t in range(TT):
                mm = nc.tensor.transpose(bank[n][:, :].bitcast(F16)[96:128, t * P:(t + 1) * P],
                                         nm[:, t, :, :].rearrange("p h i -> p (h i)"), ident16[:, :])
            mm.then_inc(bank_filled[n], 1)
            pe.wait_ge(mrow_in, it * 16 + 16)
            for h in range(H):
                for j in range(2):
                    pe.wait_ge(pair_free[j], it * 2 * H + H + h + 1)
                    for i in range(2):
                        t = 2 * j + i
                        mm = nc.tensor.matmul(pair[j][:, i, :], kT[:, h, t * P:(t + 1) * P], qT[:, h, :], start=True, stop=True)
                    mm.then_inc(pair_filled[j], 1)
                if h:
                    probs_v(it, h - 1)
            probs_v(it, H - 1)
            pe.wait_ge(o_ready, it * TT + TT)
            for k in range(KT):
                n, c = turn(it, "ot", k)
                pe.wait_ge(bank_free[n], c)
                for t in range(TT):
                    mm = nc.tensor.transpose(bank[n][:, t * P:(t + 1) * P],
                                             osb[:, t, 4 * k:4 * k + 4, :].rearrange("p h d -> p (h d)"), ident32[:, :])
                mm.then_inc(bank_filled[n], 1)
            for k in range(1, KT):
                n, c = turn(it, "ot", k)
                pe.wait_ge(bank_free[n], c + 1)
            for t in range(TT):
                project(it, ("wo", t), lambda a, k: nxT[:, a, k, t * P:(t + 1) * P], lambda b, k: wq[:, 3, b, k, :], KT, bias=(3, 1))
            norm_transposes(it, "n2", TT)
            pe.wait_ge(nx_ready, it * 2 * KT + 2 * KT)
            for part in range(2):
                for f in range(part * FH, part * FH + FH):
                    i = f % WRING
                    pe.wait_ge(wgu_in[i], (it * (FT // WRING) + f // WRING + 1) * 16)
                    project(it, ("g", f), lambda a, k: wgu[:, i, 0, a, k, :], lambda b, k: nxT[:, b, k, :], KT)
                    project(it, ("u", f), lambda a, k: wgu[:, i, 1, a, k, :], lambda b, k: nxT[:, b, k, :], KT)
                for t in range(TT):
                    wait = None
                    if t == 0:
                        wait = lambda f: pe.wait_ge(h_ready, it * FT + part * FH + f + 1)
                    project(it, ("dn", part, t), lambda a, f: hT[:, a, f, t * P:(t + 1) * P],
                            lambda b, f: wdn[:, b, part * FH + f, :], FH, wait=wait)

    def take_pv(act, it, h):
        act.wait_ge(pv_filled, it * H + h + 1)
        pv = pvb[:, 0:TT * VW].rearrange("p (t c) -> p t c", t=TT)
        nc.scalar.copy(osb[:, :, h, :], pv[:, :, 0:HD])
        nc.scalar.copy(den[:, :, h:h + 1], pv[:, :, 2 * HD:VW]).then_inc(o_copied, 1)

    @block.scalar
    def _(act):
        def norm_tiles(it, which, i):
            for k in range(KT):
                n, c = turn(it, which, k)
                act.wait_ge(bank_filled[n], c)
                if i or k >= 2:
                    act.wait_ge(nx_ready, it * 2 * KT + i * KT + k - 1)
                nc.scalar.activation(acts[:, k % 2, :], bank[n][:, :], ACT.Identity, scale=mods[:, i, 0, k:k + 1],
                                     bias=mods[:, i, 1, k:k + 1]).then_inc(bank_free[n], 1)

        with act.Fori(0, B) as it:
            act.wait_ge(x_in, it * 16 + 16)
            for t in range(TT):
                nc.scalar.activation(junk[:, :], xin[:, t, :], ACT.Square, accum_out=ssq[:, 0, t:t + 1]).then_inc(sq[0], 1)
                act.wait_ge(sq[0], it * TT + t + 1)
            for t in range(TT):
                act.wait_ge(x1_ready, it * TT + t + 1)
                nc.scalar.activation(junk[:, :], x1[:, t, :], ACT.Square, accum_out=ssq[:, 1, t:t + 1]).then_inc(sq[1], 1)
                act.wait_ge(sq[1], it * TT + t + 1)
            act.wait_ge(mods_in, it * 16 + 16)
            norm_tiles(it, "n1", 0)

            def q_copy(t):
                for g in range(2):
                    n, c = turn(it, "st", t, "q", g)
                    act.wait_ge(bank_filled[n], c)
                    nc.scalar.copy(qT[0:96, 8 * g:8 * g + 8, t * P:(t + 1) * P],
                                   bank[n][:, :].bitcast(F16)[0:96, :].rearrange("p (h s) -> p h s", h=8)).then_inc(bank_free[n], 1)

            for t in range(TT):
                n, c = turn(it, "qkv", t, "v")
                act.wait_ge(bank_filled[n], c)
                nc.scalar.copy(v[:, t, :, 0:HD], bank[n][:, :].rearrange("p (h d) -> p h d", h=H)).then_inc(v_hi, 1)
                if t:
                    q_copy(t - 1)
                for m, name in enumerate("qk"):
                    act.wait_ge(rope_sum, it * 2 * TT + 2 * t + m + 1)
                    if t:
                        n, c = turn(it, "st", t - 1, name, 1)
                        act.wait_ge(bank_filled[n], c)
                    blocks = stack[:, m, :, :].rearrange("p h (c j) -> p h c j", c=3)
                    dst = blocks[:, :, 0:2, :] if m == 0 else blocks[:, :, 0:3:2, :]
                    src = rt[:, m, 0, :].rearrange("p (h o j) -> p h o j", h=H, o=1).to_broadcast([P, H, 2, HD])
                    nc.scalar.copy(dst, src).then_inc(rope_hi, 1)
            q_copy(TT - 1)
            for h in range(H):
                for j in range(2):
                    act.wait_ge(pair_filled[j], it * 2 * H + H + h + 1)
                    if h:
                        act.wait_ge(p_ready, it * 2 * H + 2 * h + j - 1)
                    nc.scalar.activation(p32[:, j, :, :], pair[j][:, :, :], ACT.Exp, scale=INV_SQRT_HD).then_inc(pair_free[j], 1)
                if h:
                    take_pv(act, it, h - 1)
            take_pv(act, it, H - 1)
            for k in range(KT):
                n, c = turn(it, "ot", k)
                act.wait_ge(bank_filled[n], c)
                nc.scalar.copy(nxT[:, 0, k, :], bank[n][:, :]).then_inc(ot_hi, 1)
            for t in range(TT):
                n, c = turn(it, "wo", t)
                act.wait_ge(bank_free[n], c + 1)
                nc.scalar.activation(junk[:, :], x1[:, t, :], ACT.Square, accum_out=ssq[:, 2, t:t + 1]).then_inc(sq[2], 1)
                act.wait_ge(sq[2], it * TT + t + 1)
            norm_tiles(it, "n2", 1)
            for part in range(2):
                for f in range(part * FH, part * FH + FH + 1):
                    if f < part * FH + FH:
                        n, c = turn(it, "g", f)
                        act.wait_ge(bank_filled[n], c)
                        if f < 2:
                            act.wait_ge(nx_ready, it * 2 * KT + 2 * KT + f - 1)
                        else:
                            m, d = turn(it, "u", f - 2)
                            act.wait_ge(bank_free[m], d + 1)
                        nc.scalar.activation(acts[:, f % 2, :], bank[n][:, :], ACT.Gelu, scale=UNSCALE).then_inc(bank_free[n], 1)
                    if f > part * FH:
                        n, c = turn(it, "u", f - 1)
                        act.wait_ge(bank_free[n], c + 1)
                        if f == FH + 1:
                            m, d = turn(it, "dn", 0, TT - 1)
                            act.wait_ge(bank_filled[m], d)
                        nc.scalar.copy(hT[:, 0, (f - 1) % FH, :], hf[:, (f - 1) % 2, :]).then_inc(h_hi, 1)

    @block.vector
    def _(dve):
        def norm_split(it, which, i):
            for k in range(KT):
                u = i * KT + k
                n, c = turn(it, which, k)
                dve.wait_ge(bank_free[n], c + 1)
                nc.vector.tensor_copy(nxT[:, 0, k, :], acts[:, u % 2, :]).then_inc(nx_hi, 1)
                dve.wait_ge(nx_hi, it * 2 * KT + u + 1)
                nc.vector.tensor_tensor(nxT[:, 1, k, :], acts[:, u % 2, :], nxT[:, 0, k, :], ALU.subtract).then_inc(nx_ready, 1)

        def k_copy(it, t):
            for g in range(2):
                n, c = turn(it, "st", t, "k", g)
                dve.wait_ge(bank_filled[n], c)
                nc.vector.tensor_copy(kT[0:96, 8 * g:8 * g + 8, t * P:(t + 1) * P],
                                      bank[n][:, :].bitcast(F16)[0:96, :].rearrange("p (h s) -> p h s", h=8)).then_inc(bank_free[n], 1)

        with dve.Fori(0, B) as it:
            dve.wait_ge(x_in, it * 16 + 16)
            dve.wait_ge(rows_in, it * 16 + 16)
            dve.wait_ge(inv_ready[0], it + 1)
            dve.wait_ge(stored, it * 16 * TT + 1)
            for t in range(TT):
                nc.vector.scalar_tensor_tensor(out=x1[:, t, :], in0=xin[:, t, :], scalar=inv[:, 0, t:t + 1], in1=rows[:, 0, :],
                                               op0=ALU.mult, op1=ALU.mult).then_inc(x1a, 1)
            for t in range(TT):
                dve.wait_ge(x1a, it * TT + t + 1)
                nc.vector.tensor_tensor(x1[:, t, :], x1[:, t, :], rows[:, 1, :], ALU.add).then_inc(x1_ready, 1)
            dve.wait_ge(inv_ready[1], it + 1)
            for t in range(TT):
                nc.vector.tensor_scalar(xin[:, t, :], x1[:, t, :], inv[:, 1, t:t + 1], None, ALU.mult).then_inc(xn_ready, 1)
            norm_split(it, "n1", 0)

            for t in range(TT):
                for m, name in enumerate("qk"):
                    n, c = turn(it, "qkv", t, name)
                    dve.wait_ge(bank_filled[n], c)
                    q = bank[n][:, :].rearrange("p (h c j) -> p h c j", h=H, c=2)
                    r = rt[:, m, :, :].rearrange("p i (h c j) -> p i h c j", h=H, c=2)
                    tab = rope[:, t, :, :].rearrange("p a (o c j) -> p a o c j", o=1, c=2)
                    if t:
                        dve.wait_ge(rope_ready, it * 2 * TT + 2 * (t - 1) + m + 1)
                    nc.vector.tensor_tensor(rt[:, m, 0, :].rearrange("p (h j) -> p h j", h=H), bank[n][:, :].rearrange("p (h j) -> p h j", h=H),
                                            rope[:, t, 0:1, :].to_broadcast([P, H, HD]), ALU.mult)
                    for a in range(2):
                        ins = nc.vector.tensor_tensor(r[:, 1, :, a, :], q[:, :, 1 - a, :],
                                                      tab[:, 1, :, a, :].to_broadcast([P, H, HD // 2]), ALU.mult)
                    ins.then_inc(bank_free[n], 1)
                    dve.wait_ge(bank_free[n], c + 1)
                    nc.vector.tensor_tensor(rt[:, m, 0, :], rt[:, m, 0, :], rt[:, m, 1, :], ALU.add).then_inc(rope_sum, 1)
                n, c = turn(it, "qkv", t, "v")
                dve.wait_ge(v_hi, it * TT + t + 1)
                nc.vector.tensor_tensor(v[:, t, :, HD:2 * HD], bank[n][:, :].rearrange("p (h d) -> p h d", h=H),
                                        v[:, t, :, 0:HD], ALU.subtract).then_inc(bank_free[n], 1)
                if t:
                    k_copy(it, t - 1)
                for m in range(2):
                    dve.wait_ge(rope_hi, it * 2 * TT + 2 * t + m + 1)
                    lo = 2 * HD if m == 0 else HD
                    nc.vector.tensor_tensor(stack[:, m, :, lo:lo + HD], rt[:, m, 0, :].rearrange("p (h j) -> p h j", h=H),
                                            stack[:, m, :, 0:HD], ALU.subtract).then_inc(rope_ready, 1)
            k_copy(it, TT - 1)
            for h in range(H):
                for j in range(2):
                    dve.wait_ge(pair_filled[j], it * 2 * H + h + 1)
                    nc.vector.tensor_reduce(mx[:, h, 2 * j:2 * j + 2], pair[j][:, :, :], AX_X, ALU.max).then_inc(pair_free[j], 1)
                    mx_last = it * 2 * H + h + 2
            for j in range(2):
                dve.wait_ge(pair_free[j], mx_last)
            nc.vector.tensor_scalar(nmf[:, :, :], mx[:, :, :].rearrange("p h t -> p t h"), -1.0, LN_SCALE * float(HD) ** 0.5,
                                    ALU.mult, ALU.add).then_inc(nm_step, 1)
            dve.wait_ge(nm_step, it * 2 + 1)
            nc.vector.tensor_copy(nm[:, :, :, 0], nmf[:, :, :]).then_inc(nm_step, 1)
            dve.wait_ge(nm_step, it * 2 + 2)
            nc.vector.tensor_tensor(nm[:, :, :, 1], nmf[:, :, :], nm[:, :, :, 0], ALU.subtract).then_inc(nm_ready, 1)
            n, c = turn(it, "mt")
            dve.wait_ge(bank_filled[n], c)
            nc.vector.tensor_copy(mrow[96:128, :], bank[n][:, :].bitcast(F16)[96:128, 0:S]).then_inc(bank_free[n], 1)

            def add_pv(h):
                dve.wait_ge(o_copied, it * H + h + 1)
                pv = pvb[:, 0:TT * VW].rearrange("p (t c) -> p t c", t=TT)
                nc.vector.tensor_tensor(osb[:, :, h, :], osb[:, :, h, :], pv[:, :, HD:2 * HD], ALU.add).then_inc(pv_free, 1)

            for h in range(H):
                for j in range(2):
                    if j == 0 and h >= 2:
                        dve.wait_ge(pv_filled, it * H + h - 1)
                    dve.wait_ge(pair_free[j], it * 2 * H + H + h + 2)
                    hi = front[:, h % 2, 0, j * 2 * S:(j + 1) * 2 * S]
                    lo = front[:, h % 2, 1, j * 2 * S:(j + 1) * 2 * S]
                    src = p32[:, j, :, :].rearrange("p k s -> p (k s)")
                    nc.vector.tensor_copy(hi, src).then_inc(p_hi, 1)
                    dve.wait_ge(p_hi, it * 2 * H + 2 * h + j + 1)
                    nc.vector.tensor_tensor(lo, src, hi, ALU.subtract).then_inc(p_ready, 1)
                if h >= 2:
                    add_pv(h - 2)
            add_pv(H - 2)
            add_pv(H - 1)
            nc.vector.reciprocal(rden[:, :, :], den[:, :, :]).then_inc(rden_ready, 1)
            dve.wait_ge(rden_ready, it + 1)
            dve.wait_ge(pv_free, it * H + H + 1)
            for t in range(TT):
                nc.vector.tensor_tensor(osb[:, t, :, :], osb[:, t, :, :],
                                        rden[:, t, :].rearrange("p (h o) -> p h o", o=1).to_broadcast([P, H, HD]), ALU.mult).then_inc(o_ready, 1)
            for k in range(KT):
                n, c = turn(it, "ot", k)
                dve.wait_ge(ot_hi, it * KT + k + 1)
                nc.vector.tensor_tensor(nxT[:, 1, k, :], bank[n][:, :], nxT[:, 0, k, :], ALU.subtract).then_inc(bank_free[n], 1)
            for t in range(TT):
                n, c = turn(it, "wo", t)
                dve.wait_ge(bank_filled[n], c)
                nc.vector.scalar_tensor_tensor(out=x1[:, t, :], in0=bank[n][:, :], scalar=UNSCALE * UNSCALE, in1=x1[:, t, :],
                                               op0=ALU.mult, op1=ALU.add).then_inc(bank_free[n], 1)
            dve.wait_ge(inv_ready[2], it + 1)
            for t in range(TT):
                nc.vector.tensor_scalar(xin[:, t, :], x1[:, t, :], inv[:, 2, t:t + 1], None, ALU.mult).then_inc(xn_ready, 1)
            norm_split(it, "n2", 1)
            dve.wait_ge(nx_ready, it * 2 * KT + 2 * KT)
            dve.sem_inc(xin_free, 1)
            for part in range(2):
                for f in range(part * FH, part * FH + FH + 1):
                    if f < part * FH + FH:
                        n, c = turn(it, "u", f)
                        m, d = turn(it, "g", f)
                        dve.wait_ge(bank_free[m], d + 1)
                        dve.wait_ge(bank_filled[n], c)
                        if f >= 2:
                            dve.wait_ge(h_ready, it * FT + f - 1)
                        nc.vector.tensor_tensor(hf[:, f % 2, :], bank[n][:, :], acts[:, f % 2, :], ALU.mult).then_inc(bank_free[n], 1)
                    if f > part * FH:
                        dve.wait_ge(h_hi, it * FT + f)
                        nc.vector.tensor_tensor(hT[:, 1, (f - 1) % FH, :], hf[:, (f - 1) % 2, :], hT[:, 0, (f - 1) % FH, :],
                                                ALU.subtract).then_inc(h_ready, 1)
                for t in range(TT):
                    n, c = turn(it, "dn", part, t)
                    dve.wait_ge(bank_filled[n], c)
                    nc.vector.scalar_tensor_tensor(out=x1[:, t, :], in0=bank[n][:, :], scalar=UNSCALE * UNSCALE, in1=x1[:, t, :],
                                                   op0=ALU.mult, op1=ALU.add).then_inc(bank_free[n], 1)


def block_kernel(nc, w, out):
    with ExitStack() as ctx:
        def sb(name, shape, dt):
            return ctx.enter_context(nc.sbuf_tensor(name, shape, dt))

        def sem(name):
            return ctx.enter_context(nc.semaphore(name))

        res = {
            "wqkvo": sb("wqkvo", [P, 4, 2, KT, 512], F16),
            "wdn": sb("wdn", [P, 2, FT, 512], F16),
            "ident16": sb("ident16", [P, P], F16),
            "ident32": sb("ident32", [P, P], F32),
            "rope": sb("rope", [P, TT, 2, HD], F32),
            "kT": sb("kT", [P, H, S], F16),
            "v": sb("v", [P, TT, H, VW], F16),
            "brow": sb("brow", [P, 4, 512], F16),
            "bones": sb("bones", [P, 2, P], F16),
            "bank_free": [sem(f"bank{k}_free") for k in range(RING)],
            "pair_free": [sem(f"pair{j}_free") for j in range(2)],
            "pv_free": sem("pv_free"), "xin_free": sem("xin_free"), "stored": sem("stored"),
        }
        res["free"] = [*res["bank_free"], *res["pair_free"], res["pv_free"], res["xin_free"], res["stored"]]
        scratch = {
            "gu": nc.dram_tensor("gu_split", (FT, P, 2, 2, KT, P), F16).ap(),
            "rows": nc.dram_tensor("rows_all", (B, 1024), F32).ap(),
            "mods": nc.dram_tensor("mods_all", (B, P, 4 * KT), F32).ap(),
        }
        with ExitStack() as inner:
            prepare(nc, inner, w, res, scratch)
        with ExitStack() as inner:
            sequences(nc, inner, w, res, scratch, out)


_INS = {
    "x": "x", "cond_1024": "cond", "L0_cond_w_proj": "w_proj", "L0_cond_b_proj": "b_proj", "L0_cond_rms_weight": "rms_weight",
    "L1_cond_t1_w1": "t1_w1", "L1_cond_t1_w2": "t1_w2", "L1_cond_t2_w1": "t2_w1", "L1_cond_t2_w2": "t2_w2",
    "L1_cond_wq": "wq", "L1_cond_bq": "bq", "L1_cond_wk": "wk", "L1_cond_bk": "bk", "L1_cond_wv": "wv", "L1_cond_bv": "bv",
    "L1_cond_wo": "wo", "L1_cond_bo": "bo", "L1_cond_w_gate": "w_gate", "L1_cond_w_up": "w_up", "L1_cond_w_down": "w_down",
}


def _constants():
    import numpy as np
    freq = (np.float32(1.0) / np.float32(10000.0) ** (np.arange(0, 32, 2, dtype=np.float32) / np.float32(32))).astype(np.float32)
    angle = np.arange(512, dtype=np.float32)[:, None] * freq[None, :]
    c, s = np.cos(angle), np.sin(angle)
    rope = np.stack([np.concatenate([c, c], 1), np.concatenate([-s, s], 1)], 1).astype(np.float32) / np.float32(256)
    pick = (np.arange(32)[:, None] // 2 == np.arange(16)[None, :]).astype(np.float16)
    return {"ident16": np.eye(128, dtype=np.float16), "ident32": np.eye(128, dtype=np.float32), "rope": rope, "pick": pick}


def _by_features(inputs):
    import numpy as np
    cols = lambda name: np.asarray(inputs["L1_cond_" + name]).reshape(-1, 128).T
    vecs = [np.concatenate([cols(f"t{i}_b1"), cols(f"t{i}_b2"), cols(f"w_norm{i}")], 1) for i in (1, 2)]
    cond_t = np.asarray(inputs["cond_1024"]).T.reshape(4, 128, 8).transpose(1, 0, 2)
    return {"vecs": np.stack(vecs, 1), "cond_t": cond_t}


def kernel(**inputs):
    import numpy as _np
    import concourse.bacc as _bacc
    from concourse import mybir as _mybir
    from concourse.bass_utils import run_bass_kernel_spmd as _run

    nc = _bacc.Bacc("TRN2", target_bir_lowering=False, num_devices=1)
    arrays, aps = {}, {}
    named = [(_INS[k], inputs[k]) for k in _INS] + list(_constants().items()) + list(_by_features(inputs).items())
    for name, value in named:
        a = _np.ascontiguousarray(value)
        arrays[f"in_{name}_dram"] = a
        aps[name] = nc.dram_tensor(f"in_{name}_dram", a.shape, _mybir.dt.from_np(a.dtype), kind="ExternalInput").ap()
    out = nc.dram_tensor("out_0_dram", (8, 512, 512), _mybir.dt.float32, kind="ExternalOutput").ap()
    block_kernel(nc, aps, out)
    r = _run(nc, [arrays], core_ids=[0])
    return r.results[0]["out_0_dram"]
```

```python
from contextlib import ExitStack

import concourse.bass as bass
from concourse import mybir

ALU = mybir.AluOpType
ACT = mybir.ActivationFunctionType
F32 = mybir.dt.float32
F16 = mybir.dt.float16
AX_X = mybir.AxisListType.X

P = 128
B, S, D = 8, 512, 512
H, HD = 16, 32
F = 2048
TT = S // P
KT = D // P
FT = F // P
FH = FT // 2
W_SCALE = 256.0
SQRT_D = float(D) ** 0.5
UNSCALE = 1.0 / W_SCALE
LN_SCALE = 8 * 0.6931471805599453
RING = 3
WRING = 2
VW = 2 * HD + 1


def front_qkv():
    steps = []
    for t in range(TT):
        steps += [("qkv", t, m) for m in "qkv"]
        if t:
            steps += [("st", t - 1, m, g) for m in "qk" for g in range(2)]
    return steps + [("st", TT - 1, m, g) for m in "qk" for g in range(2)]


def bank_turns(front, back):
    steps = []
    if back:
        steps += [("ot", k) for k in range(KT)] + [("wo", t) for t in range(TT)] + [("n2", k) for k in range(KT)]
        steps += [(p, f) for f in range(FH) for p in "gu"] + [("dn", 0, 0), ("dn", 0, 1)]
    if front:
        steps += [("n1", k) for k in range(KT)]
    if back:
        steps += [("dn", 0, 2), ("dn", 0, 3)]
    if front:
        steps += front_qkv()
    if back:
        steps += [(p, f) for f in range(FH, FT) for p in "gu"] + [("dn", 1, 0)]
    if front:
        steps += [("mt",)]
    if back:
        steps += [("dn", 1, t) for t in range(1, TT)]
    return {step: n for n, step in enumerate(steps)}


class Body:
    FIRST, LOOP, LAST = bank_turns(True, False), bank_turns(True, True), bank_turns(False, True)

    def __init__(self, it=None, front=None, back=None):
        self.front, self.back = front, back
        self.turns = {(True, False): Body.FIRST, (True, True): Body.LOOP, (False, True): Body.LAST}[
            front is not None, back is not None]
        self.it = it

    @staticmethod
    def count(turns, k):
        return len(range(k, len(turns), RING))

    def turn(self, *step):
        n = self.turns[step]
        k = n % RING
        before = 0 if self.back is None else Body.count(Body.FIRST, k) + self.it * Body.count(Body.LOOP, k)
        return k, before + n // RING + 1


def bodies(engine, program):
    program(Body(front=0))
    with engine.Fori(0, B - 1) as it:
        program(Body(it=it, front=it + 1, back=it))
    program(Body(it=B - 1, back=B - 1))


def prepare(nc, ctx, w, res, scratch):
    def sb(name, shape, dt=F32):
        return ctx.enter_context(nc.sbuf_tensor(name, shape, dt))

    def sem(name):
        return ctx.enter_context(nc.semaphore(name))

    stage = sb("p_stage", [P, 3, 2048])
    hi_out = sb("p_hi", [P, 2, 2048], F16)
    lo_out = sb("p_lo", [P, 2, 2048], F16)
    cond = sb("p_cond", [B, D])
    cond_t = sb("p_cond_t", [P, KT, B])
    wp = sb("p_wp", [P, 8, 512])
    tern = sb("p_tern", [P, 8, 512], F16)
    tern_t = sb("p_tern_t", [P, KT, 1024], F16)
    pick = sb("p_pick", [P, H], F16)
    absum = sb("p_absum", [P, 1])
    mean = sb("p_mean", [P, 1])
    wscale = sb("p_wscale", [P, 1])
    cmax = sb("p_cmax", [B, 1])
    cinv = sb("p_cinv", [B, 1])
    cfac = sb("p_cfac", [B, 1])
    cint = cond
    cint16 = sb("p_cint16", [B, D], F16)
    cint_t = sb("p_cint_t", [P, KT, B], F16)
    bproj = sb("p_bproj", [B, 1024])
    rmsw = sb("p_rmsw", [B, D])
    emb = sb("p_emb", [B, 1024])
    ones = sb("p_ones", [P, P])
    w1 = sb("p_w1", [P, KT, 512])
    w2 = sb("p_w2", [P, KT, 1024])
    vecs = sb("p_vecs", [P, 2, 4 * KT])
    b1, b2, wn = vecs[:, :, 0:KT], vecs[:, :, KT:3 * KT], vecs[:, :, 3 * KT:4 * KT]
    z = sb("p_z", [P, KT, B])
    ez = sb("p_ez", [P, KT, B])
    y = sb("p_y", [P, 8, B])
    mods = sb("p_mods", [P, B, 2, 2, KT])
    bias4 = sb("p_bias4", [4, 512])
    bsplit = sb("p_bsplit", [4, 2, 512], F16)

    ps_t = ctx.enter_context(nc.psum_tensor("p_ps_t", [P, 2, 1024], F16))
    ps_e = ctx.enter_context(nc.psum_tensor("p_ps_e", [P, 2, 512], F32))
    ps_s = ctx.enter_context(nc.psum_tensor("p_ps_s", [P, 512], F32))
    ps_m = ctx.enter_context(nc.psum_tensor("p_ps_m", [P, 512], F32))

    staged = [sem(f"p_staged{i}") for i in range(3)]
    hi_done, lo_done = sem("p_hi_done"), sem("p_lo_done")
    kept = [sem("p_kept0"), sem("p_kept1")]
    small, wp_in, w12_in = sem("p_small"), sem("p_wp_in"), sem("p_w12_in")
    consts_in = sem("p_consts_in")
    v = sem("p_vector_step")
    abs_done, tr_done, tr_free = sem("p_abs_done"), sem("p_tr_done"), sem("p_tr_free")
    sum_done, emb_done, emb_out = sem("p_sum_done"), sem("p_emb_done"), sem("p_emb_out")
    ones_set = sem("p_ones_set")
    mlp1, mlp2, sil = sem("p_mlp1"), sem("p_mlp2"), sem("p_silu")
    z_ready, h_ready, y_used = sem("p_z_ready"), sem("p_h_ready"), sem("p_y_used")
    mods_ready, mods_out = sem("p_mods_ready"), sem("p_mods_out")
    bias_in, bias_hi, brow_in = sem("p_bias_in"), sem("p_bias_hi"), sem("p_brow_in")

    units = []
    for m, name in enumerate(["wq", "wk", "wv", "wo"]):
        units.append((w[name].rearrange("(k p) n -> p k n", p=P), ("qkvo", m)))
    for g, name in enumerate(["w_gate", "w_up"]):
        for k in range(KT):
            units.append((w[name][k * P:(k + 1) * P, :], ("gu", g, k)))
    for c in range(4):
        units.append((w["w_down"][c * 512:(c + 1) * 512, :].rearrange("(f p) n -> p f n", p=P), ("dn", c)))
    order = units[:4] + units[4:]
    n_gu = [n for n, u in enumerate(order) if u[1][0] == "gu"]

    def place(n):
        kind = order[n][1]
        if kind[0] == "qkvo":
            return [res["wqkvo"][:, kind[1], i, :, :] for i in range(2)]
        if kind[0] == "dn":
            return [res["wdn"][:, i, 4 * kind[1]:4 * kind[1] + 4, :] for i in range(2)]
        j = n_gu.index(n) % 2
        return [x[:, j, :] for x in (hi_out, lo_out)]

    def staging(n):
        ap = stage[:, n % 3, :]
        if order[n][1][0] != "gu":
            ap = ap.rearrange("p (k n) -> p k n", k=4)
        return ap

    def put_copy(sp, n):
        _, g, k = order[n][1]
        j = n_gu.index(n)
        sp.wait_ge(lo_done, n + 1)
        for i, src in enumerate((hi_out, lo_out)):
            dst = scratch["gu"][:, :, g, i, k, :].rearrange("f p n -> p f n")
            sp.dma_start(dst, src[:, j % 2, :].rearrange("p (f n) -> p f n", f=FT)).then_inc(kept[j % 2], 16)

    block = ctx.enter_context(nc.Block())

    @block.sync
    def _(sp):
        sp.dma_start(res["ident16"][:, :], w["ident16"]).then_inc(consts_in, 16)
        sp.dma_start(res["ident32"][:, :], w["ident32"]).then_inc(consts_in, 16)
        sp.dma_start(res["rope"][:, :, :, :], w["rope"].rearrange("(t p) c j -> p t c j", p=P)).then_inc(consts_in, 16)
        sp.dma_start(pick[96:128, :], w["pick"]).then_inc(consts_in, 16)
        sp.dma_start(res["bones"][:, :, :], w["bones"]).then_inc(consts_in, 16)
        for n, (src, _) in enumerate(order):
            if n >= 3:
                sp.wait_ge(lo_done, n - 2)
            sp.dma_start(staging(n), src).then_inc(staged[n % 3], 16)
            if n >= 2 and n - 2 in n_gu:
                put_copy(sp, n - 2)
        for n in range(len(order) - 2, len(order)):
            if n in n_gu:
                put_copy(sp, n)
        sp.wait_ge(mods_ready, 4)
        sp.dma_start(scratch["mods"].rearrange("b p c -> p b c"),
                     mods[:, :, :, :, :].rearrange("p b s a k -> p b (s a k)")).then_inc(mods_out, 16)
        sp.wait_ge(mods_out, 16)
        sp.wait_ge(kept[0], 16 * len(n_gu))
        sp.wait_ge(kept[1], 16 * len(n_gu))

    @block.gpsimd
    def _(pool):
        nc.gpsimd.memset(ones[:, :], 1.0).then_inc(ones_set, 1)
        pool.dma_start(wp[:, :, :], w["w_proj"].rearrange("(r p) c -> p r c", p=P)).then_inc(wp_in, 16)
        pool.dma_start(cond[:, :], w["cond"]).then_inc(small, 16)
        pool.dma_start(bproj[:, :], w["b_proj"].rearrange("(o n) -> o n", o=1).to_broadcast([B, 1024])).then_inc(small, 16)
        pool.dma_start(rmsw[:, :], w["rms_weight"].rearrange("(o n) -> o n", o=1).to_broadcast([B, D])).then_inc(small, 16)
        pool.dma_start(cond_t[:, :, :], w["cond_t"]).then_inc(small, 16)
        pool.dma_start(vecs[:, :, :], w["vecs"]).then_inc(small, 16)
        for m, name in enumerate(["bq", "bk", "bv", "bo"]):
            pool.dma_start(bias4[m:m + 1, :], w[name].rearrange("(o n) -> o n", o=1)).then_inc(bias_in, 16)
        for i in range(2):
            if i:
                pool.wait_ge(mlp2, 1)
            pool.dma_start(w1[:, :, :], w[f"t{i+1}_w1"].rearrange("(k p) n -> p k n", p=P)).then_inc(w12_in, 16)
            pool.dma_start(w2[:, :, :], w[f"t{i+1}_w2"].rearrange("(k p) n -> p k n", p=P)).then_inc(w12_in, 16)
        pool.wait_ge(v, 4)
        for i in range(2):
            pool.dma_start(res["brow"][4 * i:4 * i + 4, :], bsplit[:, i, :]).then_inc(brow_in, 16)
        pool.wait_ge(brow_in, 32)
        pool.wait_ge(v, 17)
        pool.dma_start(scratch["rows"], emb[:, :]).then_inc(emb_out, 16)
        pool.wait_ge(emb_out, 16)

    @block.scalar
    def _(act):
        act.wait_ge(wp_in, 16)
        nc.scalar.activation(tern[:, :, :], wp[:, :, :], ACT.Abs, accum_out=absum[:, :]).then_inc(abs_done, 1)
        for n in range(len(order)):
            act.wait_ge(staged[n % 3], 16 * (n // 3 + 1))
            if n in n_gu and n_gu.index(n) >= 2:
                j = n_gu.index(n)
                act.wait_ge(kept[j % 2], 32 * (j // 2))
            nc.scalar.activation(place(n)[0], staging(n), ACT.Copy, scale=W_SCALE).then_inc(hi_done, 1)
            if n in (3, 9):
                i = int(n == 9)
                act.wait_ge(z_ready, i + 1)
                nc.scalar.activation(ez[:, :, :], z[:, :, :], ACT.Exp, scale=-1.0).then_inc(sil, 1)

    @block.tensor
    def _(pe):
        pe.wait_ge(consts_in, 80)
        pe.wait_ge(ones_set, 1)
        pe.wait_ge(abs_done, 1)
        nc.tensor.matmul(ps_s[:, 0:1], ones[:, :], absum[:, :], start=True, stop=True).then_inc(sum_done, 1)
        for i in range(2):
            pe.wait_ge(small, 16 * 5)
            pe.wait_ge(w12_in, 32 * (i + 1))
            if i:
                pe.wait_ge(y_used, 1)
            for m in range(KT):
                for k in range(KT):
                    mm = nc.tensor.matmul(ps_m[:, m * B:(m + 1) * B], w1[:, k, m * P:(m + 1) * P], cond_t[:, k, :],
                                          start=(k == 0), stop=(k == KT - 1))
            mm.then_inc(mlp1, 1)
            pe.wait_ge(h_ready, i + 1)
            for m in range(8):
                for k in range(KT):
                    mm = nc.tensor.matmul(ps_m[:, 64 + m * B:64 + (m + 1) * B], w2[:, k, m * P:(m + 1) * P], z[:, k, :],
                                          start=(k == 0), stop=(k == KT - 1))
            mm.then_inc(mlp2, 1)
        pe.wait_ge(v, 8)
        for k in range(KT):
            if k >= 2:
                pe.wait_ge(tr_free, k - 1)
            for r in range(8):
                mm = nc.tensor.transpose(ps_t[:, k % 2, r * P:(r + 1) * P], tern[:, r, k * P:(k + 1) * P], res["ident16"][:, :])
            mm.then_inc(tr_done, 1)
        pe.wait_ge(v, 12)
        pe.wait_ge(tr_free, 3)
        for k in range(KT):
            mm = nc.tensor.transpose(ps_t[:, 0, k * B:(k + 1) * B], cint16[:, k * P:(k + 1) * P], res["ident16"][0:B, 0:B])
        mm.then_inc(tr_done, 1)
        pe.wait_ge(tr_free, 5)
        for c in range(2):
            for k in range(KT):
                mm = nc.tensor.matmul(ps_e[0:B, c, :], cint_t[:, k, :], tern_t[:, k, c * 512:(c + 1) * 512],
                                      start=(k == 0), stop=(k == KT - 1))
        mm.then_inc(emb_done, 1)

    @block.vector
    def _(dve):
        n_step = [0]

        def then(ins):
            n_step[0] += 1
            ins.then_inc(v, 1)
            dve.wait_ge(v, n_step[0])

        def split_lo(n):
            dve.wait_ge(hi_done, n + 1)
            hi, lo = place(n)
            nc.vector.scalar_tensor_tensor(out=lo, in0=staging(n), scalar=W_SCALE, in1=hi,
                                           op0=ALU.mult, op1=ALU.subtract).then_inc(lo_done, 1)

        nc.vector.memset(res["brow"][:, :], 0.0)
        then(nc.vector.memset(res["v"][:, :, :, 2 * HD:VW], 1.0))
        dve.wait_ge(consts_in, 80)
        then(nc.vector.tensor_copy(res["kT"][96:128, :, :], pick[96:128, :].rearrange("p (h o) -> p h o", o=1).to_broadcast([32, H, S])))
        dve.wait_ge(bias_in, 16 * 4)
        then(nc.vector.tensor_scalar(bsplit[:, 0, :], bias4[:, :], W_SCALE, None, ALU.mult))
        then(nc.vector.scalar_tensor_tensor(out=bsplit[:, 1, :], in0=bias4[:, :], scalar=W_SCALE,
                                            in1=bsplit[:, 0, :], op0=ALU.mult, op1=ALU.subtract))
        magic = 12582912.0
        dve.wait_ge(sum_done, 1)
        then(nc.vector.tensor_scalar(mean[:, :], ps_s[:, 0:1], 1.0 / (1024 * 512), 1e-5, ALU.mult, ALU.max))
        then(nc.vector.reciprocal(wscale[:, :], mean[:, :]))
        then(nc.vector.tensor_scalar(wp[:, :, :], wp[:, :, :], wscale[:, 0:1], magic, ALU.mult, ALU.add))
        for n in range(2):
            split_lo(n)
        then2 = nc.vector.tensor_scalar(wp[:, :, :], wp[:, :, :], -magic, -1.0, ALU.add, ALU.max)
        then2.then_inc(bias_hi, 1)
        dve.wait_ge(bias_hi, 1)
        then(nc.vector.tensor_scalar(tern[:, :, :], wp[:, :, :], 1.0, None, ALU.min))
        split_lo(2)
        dve.wait_ge(small, 16 * 5)
        then(nc.vector.tensor_reduce(cmax[:, :], cond[:, :], AX_X, ALU.max, apply_absolute_value=True))
        nc.vector.tensor_scalar(cmax[:, :], cmax[:, :], 1e-5, None, ALU.max).then_inc(bias_hi, 1)
        dve.wait_ge(bias_hi, 2)
        then(nc.vector.reciprocal(cinv[:, :], cmax[:, :]))
        nc.vector.tensor_scalar(cinv[:, :], cinv[:, :], 127.0, None, ALU.mult).then_inc(bias_hi, 1)
        dve.wait_ge(bias_hi, 3)
        then(nc.vector.tensor_scalar(cint[:, :], cond[:, :], cinv[:, 0:1], magic, ALU.mult, ALU.add))
        nc.vector.tensor_scalar(cint[:, :], cint[:, :], -magic, -128.0, ALU.add, ALU.max).then_inc(bias_hi, 1)
        dve.wait_ge(bias_hi, 4)
        then(nc.vector.tensor_scalar(cint16[:, :], cint[:, :], 127.0, None, ALU.min))
        then(nc.vector.tensor_scalar(cfac[:, :], cmax[:, :], 1.0 / 127.0, mean[0:B, 0:1], ALU.mult, ALU.mult))
        for i in range(2):
            dve.wait_ge(mlp1, i + 1)
            nc.vector.tensor_tensor(z[:, :, :], ps_m[:, 0:KT * B].rearrange("p (k b) -> p k b", b=B),
                                    b1[:, i, :].rearrange("p (k o) -> p k o", o=1).to_broadcast([P, KT, B]), ALU.add).then_inc(z_ready, 1)
            if i == 0:
                split_lo(3)
            else:
                split_lo(9)
            dve.wait_ge(sil, i + 1)
            nc.vector.tensor_scalar(ez[:, :, :], ez[:, :, :], 1.0, None, ALU.add).then_inc(mods_ready, 1)
            dve.wait_ge(mods_ready, 2 * i + 1)
            nc.vector.reciprocal(ez[:, :, :], ez[:, :, :]).then_inc(bias_hi, 1)
            dve.wait_ge(bias_hi, 5 + i)
            dve.wait_ge(z_ready, i + 1)
            nc.vector.tensor_tensor(z[:, :, :], z[:, :, :], ez[:, :, :], ALU.mult).then_inc(h_ready, 1)
            if i == 0:
                for n in range(4, 7):
                    split_lo(n)
            dve.wait_ge(mlp2, i + 1)
            nc.vector.tensor_tensor(y[:, :, :], ps_m[:, 64:64 + 8 * B].rearrange("p (k b) -> p k b", b=B),
                                    b2[:, i, :].rearrange("p (k o) -> p k o", o=1).to_broadcast([P, 8, B]), ALU.add).then_inc(y_used, 1)
            dve.wait_ge(y_used, 2 * i + 1)
            nc.vector.tensor_scalar(y[:, 0:KT, :], y[:, 0:KT, :], 1.0, SQRT_D, ALU.add, ALU.mult).then_inc(y_used, 1)
            dve.wait_ge(y_used, 2 * i + 2)
            wnb = wn[:, i, :].rearrange("p (k o) -> p k o", o=1).to_broadcast([P, KT, B])
            nc.vector.tensor_tensor(mods[:, :, i, 0, :].rearrange("p b k -> p k b"), y[:, 0:KT, :], wnb, ALU.mult)
            nc.vector.tensor_copy(mods[:, :, i, 1, :].rearrange("p b k -> p k b"), y[:, KT:8, :]).then_inc(mods_ready, 1)
            if i == 0:
                for n in range(7, 9):
                    split_lo(n)
        for k in range(KT):
            dve.wait_ge(tr_done, k + 1)
            nc.vector.tensor_copy(tern_t[:, k, :], ps_t[:, k % 2, :]).then_inc(tr_free, 1)
        dve.wait_ge(tr_done, 5)
        nc.vector.tensor_copy(cint_t[:, :, :], ps_t[:, 0, 0:KT * B].rearrange("p (k b) -> p k b", b=B)).then_inc(tr_free, 1)
        for n in range(10, 13):
            split_lo(n)
        dve.wait_ge(emb_done, 1)
        for c in range(2):
            nc.vector.scalar_tensor_tensor(out=emb[:, c * 512:(c + 1) * 512], in0=ps_e[0:B, c, :], scalar=cfac[:, 0:1],
                                           in1=bproj[:, c * 512:(c + 1) * 512], op0=ALU.mult, op1=ALU.add).then_inc(v, 1)
        dve.wait_ge(v, 15)
        nc.vector.scalar_tensor_tensor(out=emb[:, 0:D], in0=emb[:, 0:D], scalar=1.0, in1=rmsw[:, :],
                                       op0=ALU.add, op1=ALU.mult).then_inc(v, 1)
        dve.wait_ge(v, 16)
        nc.vector.tensor_scalar(emb[:, 0:D], emb[:, 0:D], SQRT_D, None, ALU.mult).then_inc(v, 1)
        for n in range(13, len(order)):
            split_lo(n)
        for s in res["free"]:
            dve.sem_inc(s, 1)


def sequences(nc, ctx, w, res, scratch, out):
    def sb(name, shape, dt=F32):
        return ctx.enter_context(nc.sbuf_tensor(name, shape, dt))

    def sem(name):
        return ctx.enter_context(nc.semaphore(name))

    wq, wdn, ident16, ident32 = res["wqkvo"], res["wdn"], res["ident16"], res["ident32"]
    rope, kT, v, brow, bones = res["rope"], res["kT"], res["v"], res["brow"], res["bones"]
    bank_free, pair_free, pv_free, stored = res["bank_free"], res["pair_free"], res["pv_free"], res["stored"]

    xin = sb("xin", [P, TT, D])
    osb = xin[:, :, :].rearrange("p t (h d) -> p t h d", h=H)
    x1 = sb("x1", [P, TT, D])
    x2 = sb("x2", [P, TT, D])
    mods = sb("mods", [P, 2, 2, KT])
    ssq = sb("ssq", [P, 3, TT])
    inv = sb("inv", [P, 3, TT])
    half = sb("half", [P, TT])
    eps_d = sb("eps_d", [P, 2, TT])
    nxa = sb("nxa", [P, 2, KT, S], F16)
    nxb = sb("nxb", [P, 2, KT, S], F16)
    qT = sb("qT", [P, H, S], F16)
    wgu = sb("wgu", [P, WRING, 2, 2, KT, P], F16)
    acts = sb("acts", [P, 2, 512])
    hf = sb("hf", [P, 2, 512])
    hT = sb("hT", [P, 2, FH, S], F16)
    den = sb("den", [P, TT, H])
    rden = sb("rden", [P, TT, H])
    p32 = sb("p32", [P, 2, 2 * S])
    rows = p32[:, 0, :].rearrange("p (c d) -> p c d", c=2)
    junk = p32[:, 1, 0:D]
    front = sb("front", [P, 2, 2, TT * S], F16)
    front_flat = front[:, :, :, :].rearrange("p a b n -> p (a b n)")
    rt = front_flat[:, 0:4096].bitcast(F32).rearrange("p (m i n) -> p m i n", m=2, i=2)
    stack = front_flat[:, 4096:4096 + 2 * H * 96].rearrange("p (m h c) -> p m h c", m=2, h=H)
    mx = sb("mx", [P, H, TT])
    nmf = sb("nmf", [P, TT, H])
    nm = sb("nm", [P, TT, H, 2], F16)
    mrow = sb("mrow", [P, S], F16)

    pair = [ctx.enter_context(nc.psum_tensor(f"pair{j}", [P, 2, 512], F32)) for j in range(2)]
    pvb = ctx.enter_context(nc.psum_tensor("pvb", [P, 512], F32))
    bank = [ctx.enter_context(nc.psum_tensor(f"bank{k}", [P, 512], F32)) for k in range(RING)]
    pv = pvb[:, 0:TT * VW].rearrange("p (t c) -> p t c", t=TT)

    bank_filled = [sem(f"bank{k}_filled") for k in range(RING)]
    pair_filled = [sem(f"pair{j}_filled") for j in range(2)]
    pv_filled = sem("pv_filled")
    x_in, rows_in, mods_in = sem("x_in"), sem("rows_in"), sem("mods_in")
    wgu_in = [sem(f"wgu_in{i}") for i in range(WRING)]
    half_set = sem("half_set")
    sq = [sem(f"sq{i}") for i in range(3)]
    inv_pre, inv_ready = [sem(f"inv_pre{i}") for i in range(3)], [sem(f"inv_ready{i}") for i in range(3)]
    x1a, x1_ready = sem("x1a"), sem("x1_ready")
    xn_ready, nx_hi, nx_ready = ([sem(f"{s}{i}") for i in range(2)] for s in ("xn_ready", "nx_hi", "nx_ready"))
    rope_sum, rope_hi, rope_ready = sem("rope_sum"), sem("rope_hi"), sem("rope_ready")
    v_hi = sem("v_hi")
    nm_step, nm_ready = sem("nm_step"), sem("nm_ready")
    mrow_in = sem("mrow_in")
    p_hi, p_ready = sem("p_hi"), sem("p_ready")
    o_copied, rden_ready, o_ready = sem("o_copied"), sem("rden_ready"), sem("o_ready")
    ot_hi = sem("ot_hi")
    h_hi, h_ready = sem("h_hi"), sem("h_ready")

    PARTS = [(0, 0), (0, 1), (1, 0)]
    INV_SQRT_HD = 1.0 / float(HD) ** 0.5
    nx = [nxa, nxb]

    block = ctx.enter_context(nc.Block())

    @block.sync
    def _(sp):
        def program(body):
            f_, b = body.front, body.back

            def weights(f):
                n, c = body.turn("u", f)
                if body.front is None and f + WRING >= FT:
                    return
                sp.wait_ge(bank_filled[n], c)
                sp.dma_start(wgu[:, f % WRING, :, :, :, :], scratch["gu"][(f + WRING) % FT]).then_inc(wgu_in[f % WRING], 16)

            def store(t):
                n, c = body.turn("dn", 1, t)
                sp.wait_ge(bank_free[n], c + 1)
                sp.dma_start(out[b, t * P:(t + 1) * P, :], x2[:, t, :]).then_inc(stored, 16)

            if b is not None:
                for f in range(FT):
                    weights(f)
                store(0)
            if f_ is not None:
                n, c = body.turn("mt")
                sp.wait_ge(bank_free[n], c + 1)
                sp.dma_start(qT[96:128, :, :], mrow[96:128, :].rearrange("p (o s) -> p o s", o=1).to_broadcast([32, H, S])).then_inc(mrow_in, 16)
            if b is not None:
                for t in range(1, TT):
                    store(t)

        for f in range(WRING):
            sp.dma_start(wgu[:, f, :, :, :, :], scratch["gu"][f]).then_inc(wgu_in[f], 16)
        bodies(sp, program)
        sp.wait_ge(stored, 16 * TT * B + 1)

    @block.gpsimd
    def _(pool):
        def inverse(seq, i):
            pool.wait_ge(sq[i], seq * TT + TT)
            nc.gpsimd.tensor_tensor(ssq[:, i, :], ssq[:, i, :], eps_d[:, min(i, 1), :], ALU.add).then_inc(inv_pre[i], 1)
            pool.wait_ge(inv_pre[i], seq + 1)
            nc.gpsimd.tensor_tensor(inv[:, i, :], ssq[:, i, :], half[:, :], ALU.pow).then_inc(inv_ready[i], 1)

        def program(body):
            f_, b = body.front, body.back
            if b is not None:
                inverse(b, 2)
            if f_ is not None:
                if b is not None:
                    pool.wait_ge(nx_ready[1], b * KT + KT)
                pool.dma_start(xin[:, :, :], w["x"][f_].rearrange("(t p) d -> p t d", p=P)).then_inc(x_in, 16)
                src = scratch["rows"][0:1, :] if b is None else scratch["rows"][bass.ds(f_, 1), :]
                pool.dma_start(rows.rearrange("p c d -> p (c d)"), src.to_broadcast([P, 2 * D])).then_inc(rows_in, 16)
                pool.dma_start(mods[:, :, :, :].rearrange("p s a k -> p (s a k)"), scratch["mods"][f_]).then_inc(mods_in, 16)
                inverse(f_, 0)
                inverse(f_, 1)

        nc.gpsimd.memset(half[:, :], -0.5).then_inc(half_set, 1)
        nc.gpsimd.memset(eps_d[:, 0, :], 1e-6 * D).then_inc(half_set, 1)
        nc.gpsimd.memset(eps_d[:, 1, :], 1e-5 * D).then_inc(half_set, 1)
        pool.wait_ge(half_set, 3)
        bodies(pool, program)

    @block.tensor
    def _(pe):
        def program(body):
            f_, b = body.front, body.back

            def norm_transposes(i, which, seq):
                for k in range(KT):
                    n, c = body.turn(which, k)
                    pe.wait_ge(bank_free[n], c)
                    for t in range(TT):
                        if k == 0:
                            pe.wait_ge(xn_ready[i], seq * TT + t + 1)
                        mm = nc.tensor.transpose(bank[n][:, t * P:(t + 1) * P], xin[:, t, k * P:(k + 1) * P], ident32[:, :])
                    mm.then_inc(bank_filled[n], 1)

            def project(step, lhs, rhs, steps, bias=None, wait=None, only=None):
                n, c = body.turn(*step)
                if only is None or only[0] == 0:
                    pe.wait_ge(bank_free[n], c)
                if bias is not None:
                    nc.tensor.matmul(bank[n][:, :], bones[:, bias, :], brow[:, :], start=True, stop=False)
                for k in range(steps) if only is None else range(*only):
                    if wait is not None:
                        wait(k)
                    for p, q in PARTS:
                        mm = nc.tensor.matmul(bank[n][:, :], lhs(p, k), rhs(q, k), start=(bias is None and k == 0 and p + q == 0),
                                              stop=(k == steps - 1 and (p, q) == PARTS[-1]))
                if only is None or only[1] == steps:
                    mm.then_inc(bank_filled[n], 1)

            def stack_transposes(t):
                for m, name in enumerate("qk"):
                    pe.wait_ge(rope_ready, f_ * 2 * TT + 2 * t + m + 1)
                    for g in range(2):
                        n, c = body.turn("st", t, name, g)
                        pe.wait_ge(bank_free[n], c)
                        dst = bank[n][:, :].bitcast(F16)
                        for h in range(8):
                            mm = nc.tensor.transpose(dst[0:96, h * P:(h + 1) * P], stack[:, m, 8 * g + h, :], ident16[:, :])
                        mm.then_inc(bank_filled[n], 1)

            def gate_or_up(f, u):
                i = f % WRING
                if not u:
                    pe.wait_ge(wgu_in[i], (b * (FT // WRING) + f // WRING + 1) * 16)
                project(("gu"[u], f), lambda p, k: wgu[:, i, u, p, k, :], lambda q, k: nxb[:, q, k, :], KT)

            def down(part, t, only=None):
                wait = None
                if t == 0:
                    wait = lambda f: pe.wait_ge(h_ready, b * FT + part * FH + f + 1)
                project(("dn", part, t), lambda p, f: hT[:, p, f, t * P:(t + 1) * P],
                        lambda q, f: wdn[:, q, part * FH + f, :], FH, wait=wait, only=only)

            def scores_by_queries(h):
                for j in range(2):
                    pe.wait_ge(pair_free[j], f_ * 2 * H + h + 1)
                    for i in range(2):
                        t = 2 * j + i
                        mm = nc.tensor.matmul(pair[j][:, i, :], qT[0:96, h, t * P:(t + 1) * P], kT[0:96, h, :], start=True, stop=True)
                    mm.then_inc(pair_filled[j], 1)

            def scores_by_keys(h):
                for j in range(2):
                    pe.wait_ge(pair_free[j], f_ * 2 * H + H + h + 1)
                    for i in range(2):
                        t = 2 * j + i
                        mm = nc.tensor.matmul(pair[j][:, i, :], kT[:, h, t * P:(t + 1) * P], qT[:, h, :], start=True, stop=True)
                    mm.then_inc(pair_filled[j], 1)

            def probs_v(h):
                pe.wait_ge(p_ready, f_ * 2 * H + 2 * h + 2)
                pe.wait_ge(pv_free, f_ * H + h + 1)
                for s in range(TT):
                    for k in range(TT):
                        for a in range(2):
                            mm = nc.tensor.matmul(pvb[:, s * VW:(s + 1) * VW], front[:, h % 2, a, k * S + s * P:k * S + (s + 1) * P],
                                                  v[:, k, h, :], start=(k == 0 and a == 0), stop=(k == TT - 1 and a == 1))
                mm.then_inc(pv_filled, 1)

            if b is not None:
                pe.wait_ge(o_ready, b * TT + TT)
                for k in range(KT):
                    n, c = body.turn("ot", k)
                    pe.wait_ge(bank_free[n], c)
                    for t in range(TT):
                        mm = nc.tensor.transpose(bank[n][:, t * P:(t + 1) * P], xin[:, t, k * P:(k + 1) * P], ident32[:, :])
                    mm.then_inc(bank_filled[n], 1)
                for k in range(1, KT):
                    n, c = body.turn("ot", k)
                    pe.wait_ge(bank_free[n], c + 1)
                for t in range(TT):
                    project(("wo", t), lambda p, k: nxb[:, p, k, t * P:(t + 1) * P], lambda q, k: wq[:, 3, q, k, :], KT, bias=3)
                norm_transposes(1, "n2", b)
                pe.wait_ge(nx_ready[1], b * KT + KT)
                for f in range(FH):
                    gate_or_up(f, 0)
                    gate_or_up(f, 1)
                down(0, 0)
                down(0, 1)
            if f_ is not None:
                norm_transposes(0, "n1", f_)
            if b is not None:
                down(0, 2)
                down(0, 3)
            if f_ is not None:
                pe.wait_ge(nx_ready[0], f_ * KT + KT)
                for t in range(TT):
                    for m, name in enumerate("qkv"):
                        project(("qkv", t, name), lambda p, k: nxa[:, p, k, t * P:(t + 1) * P],
                                lambda q, k: wq[:, m, q, k, :], KT, bias=m)
                    if t:
                        stack_transposes(t - 1)
                stack_transposes(TT - 1)
                for step in [("st", TT - 1, "q", 1), ("st", TT - 1, "k", 0), ("st", TT - 1, "k", 1)]:
                    n, c = body.turn(*step)
                    pe.wait_ge(bank_free[n], c + 1)
            for h in range(H):
                if f_ is not None:
                    scores_by_queries(h)
                if b is not None:
                    gate_or_up(FH + h // 2, h % 2)
            if b is not None:
                down(1, 0)
            if f_ is not None:
                pe.wait_ge(nm_ready, f_ + 1)
                n, c = body.turn("mt")
                pe.wait_ge(bank_free[n], c)
                for t in range(TT):
                    mm = nc.tensor.transpose(bank[n][:, :].bitcast(F16)[96:128, t * P:(t + 1) * P],
                                             nm[:, t, :, :].rearrange("p h i -> p (h i)"), ident16[:, :])
                mm.then_inc(bank_filled[n], 1)
            if b is not None:
                down(1, 1)
            if f_ is not None:
                pe.wait_ge(mrow_in, f_ * 16 + 16)
            for h in range(H):
                if f_ is not None:
                    scores_by_keys(h)
                    if h:
                        probs_v(h - 1)
                if b is not None:
                    down(1, 2 + h // 8, only=(h % 8, h % 8 + 1))
            if f_ is not None:
                probs_v(H - 1)

        bodies(pe, program)

    @block.scalar
    def _(act):
        def program(body):
            f_, b = body.front, body.back

            def squares(i, seq, src, ready):
                for t in range(TT):
                    ready(t)
                    nc.scalar.activation(junk, src[:, t, :], ACT.Square, accum_out=ssq[:, i, t:t + 1]).then_inc(sq[i], 1)
                    act.wait_ge(sq[i], seq * TT + t + 1)

            def norm_tiles(i, which, seq):
                for k in range(KT):
                    n, c = body.turn(which, k)
                    act.wait_ge(bank_filled[n], c)
                    if k >= 2:
                        act.wait_ge(nx_ready[i], seq * KT + k - 1)
                    elif i == 0 and b is not None:
                        m, d = body.turn("u", FH - 2 + k)
                        act.wait_ge(bank_free[m], d + 1)
                    nc.scalar.activation(acts[:, k % 2, :], bank[n][:, :], ACT.Identity, scale=mods[:, i, 0, k:k + 1],
                                         bias=mods[:, i, 1, k:k + 1]).then_inc(bank_free[n], 1)

            def gate(f):
                n, c = body.turn("g", f)
                act.wait_ge(bank_filled[n], c)
                if f < 2:
                    act.wait_ge(nx_ready[1], b * KT + KT - 1 + f)
                elif FH <= f < FH + 2 and f_ is not None:
                    act.wait_ge(nx_ready[0], f_ * KT + KT - 1 + f - FH)
                else:
                    m, d = body.turn("u", f - 2)
                    act.wait_ge(bank_free[m], d + 1)
                nc.scalar.activation(acts[:, f % 2, :], bank[n][:, :], ACT.Gelu, scale=UNSCALE).then_inc(bank_free[n], 1)

            def h_high(f):
                n, c = body.turn("u", f)
                act.wait_ge(bank_free[n], c + 1)
                if f == FH:
                    m, d = body.turn("dn", 0, TT - 1)
                    act.wait_ge(bank_filled[m], d)
                nc.scalar.copy(hT[:, 0, f % FH, :], hf[:, f % 2, :]).then_inc(h_hi, 1)

            def q_copy(t):
                for g in range(2):
                    n, c = body.turn("st", t, "q", g)
                    act.wait_ge(bank_filled[n], c)
                    nc.scalar.copy(qT[0:96, 8 * g:8 * g + 8, t * P:(t + 1) * P],
                                   bank[n][:, :].bitcast(F16)[0:96, :].rearrange("p (h s) -> p h s", h=8)).then_inc(bank_free[n], 1)

            def take_pv(h):
                act.wait_ge(pv_filled, f_ * H + h + 1)
                nc.scalar.copy(osb[:, :, h, :], pv[:, :, 0:HD])
                nc.scalar.copy(den[:, :, h:h + 1], pv[:, :, 2 * HD:VW]).then_inc(o_copied, 1)

            def first_squares():
                squares(0, f_, xin, lambda t: act.wait_ge(x_in, f_ * 16 + 16))

            def second_squares():
                squares(1, f_, x1, lambda t: act.wait_ge(x1_ready, f_ * TT + t + 1))

            if b is not None:
                for k in range(KT):
                    n, c = body.turn("ot", k)
                    act.wait_ge(bank_filled[n], c)
                    nc.scalar.copy(nxb[:, 0, k, :], bank[n][:, :]).then_inc(ot_hi, 1)

                def wo_added(t):
                    n, c = body.turn("wo", t)
                    act.wait_ge(bank_free[n], c + 1)
                squares(2, b, x2, wo_added)
                norm_tiles(1, "n2", b)
                for f in range(FH):
                    gate(f)
                    if f:
                        h_high(f - 1)
                    if f_ is not None and f == 2:
                        first_squares()
                    if f_ is not None and f == 5:
                        second_squares()
                h_high(FH - 1)
            elif f_ is not None:
                first_squares()
                second_squares()
            if f_ is not None:
                act.wait_ge(mods_in, f_ * 16 + 16)
                norm_tiles(0, "n1", f_)
                for t in range(TT):
                    n, c = body.turn("qkv", t, "v")
                    act.wait_ge(bank_filled[n], c)
                    nc.scalar.copy(v[:, t, :, 0:HD], bank[n][:, :].rearrange("p (h d) -> p h d", h=H)).then_inc(v_hi, 1)
                    if t:
                        q_copy(t - 1)
                    for m, name in enumerate("qk"):
                        act.wait_ge(rope_sum, f_ * 2 * TT + 2 * t + m + 1)
                        if t:
                            n, c = body.turn("st", t - 1, name, 1)
                            act.wait_ge(bank_filled[n], c)
                        blocks = stack[:, m, :, :].rearrange("p h (c j) -> p h c j", c=3)
                        dst = blocks[:, :, 0:2, :] if m == 0 else blocks[:, :, 0:3:2, :]
                        src = rt[:, m, 0, :].rearrange("p (h o j) -> p h o j", h=H, o=1).to_broadcast([P, H, 2, HD])
                        nc.scalar.copy(dst, src).then_inc(rope_hi, 1)
                q_copy(TT - 1)
            if b is not None:
                for f in range(FH, FT):
                    gate(f)
                    if f > FH:
                        h_high(f - 1)
                h_high(FT - 1)
            if f_ is not None:
                for h in range(H):
                    for j in range(2):
                        act.wait_ge(pair_filled[j], f_ * 2 * H + H + h + 1)
                        if h:
                            act.wait_ge(p_ready, f_ * 2 * H + 2 * h + j - 1)
                        nc.scalar.activation(p32[:, j, :].rearrange("p (k s) -> p k s", k=2), pair[j][:, :, :], ACT.Exp,
                                             scale=INV_SQRT_HD).then_inc(pair_free[j], 1)
                    if h:
                        take_pv(h - 1)
                take_pv(H - 1)

        bodies(act, program)

    @block.vector
    def _(dve):
        def program(body):
            f_, b = body.front, body.back

            def normalise(i, seq, src):
                dve.wait_ge(inv_ready[i], seq + 1)
                for t in range(TT):
                    nc.vector.tensor_scalar(xin[:, t, :], src[:, t, :], inv[:, i, t:t + 1], None, ALU.mult).then_inc(xn_ready[i - 1], 1)

            def norm_split(i, which, seq):
                for k in range(KT):
                    n, c = body.turn(which, k)
                    dve.wait_ge(bank_free[n], c + 1)
                    nc.vector.tensor_copy(nx[i][:, 0, k, :], acts[:, k % 2, :]).then_inc(nx_hi[i], 1)
                    dve.wait_ge(nx_hi[i], seq * KT + k + 1)
                    nc.vector.tensor_tensor(nx[i][:, 1, k, :], acts[:, k % 2, :], nx[i][:, 0, k, :], ALU.subtract).then_inc(nx_ready[i], 1)

            def gate_by_up(f):
                n, c = body.turn("u", f)
                m, d = body.turn("g", f)
                dve.wait_ge(bank_free[m], d + 1)
                dve.wait_ge(bank_filled[n], c)
                if f >= 2:
                    dve.wait_ge(h_ready, b * FT + f - 1)
                nc.vector.tensor_tensor(hf[:, f % 2, :], bank[n][:, :], acts[:, f % 2, :], ALU.mult).then_inc(bank_free[n], 1)

            def h_low(f):
                dve.wait_ge(h_hi, b * FT + f + 1)
                nc.vector.tensor_tensor(hT[:, 1, f % FH, :], hf[:, f % 2, :], hT[:, 0, f % FH, :], ALU.subtract).then_inc(h_ready, 1)

            def add(step, t, src):
                n, c = body.turn(*step)
                dve.wait_ge(bank_filled[n], c)
                nc.vector.scalar_tensor_tensor(out=x2[:, t, :], in0=bank[n][:, :], scalar=UNSCALE * UNSCALE, in1=src[:, t, :],
                                               op0=ALU.mult, op1=ALU.add).then_inc(bank_free[n], 1)

            def k_copy(t):
                for g in range(2):
                    n, c = body.turn("st", t, "k", g)
                    dve.wait_ge(bank_filled[n], c)
                    nc.vector.tensor_copy(kT[0:96, 8 * g:8 * g + 8, t * P:(t + 1) * P],
                                          bank[n][:, :].bitcast(F16)[0:96, :].rearrange("p (h s) -> p h s", h=8)).then_inc(bank_free[n], 1)

            def modulate(part):
                if part == 0:
                    dve.wait_ge(x_in, f_ * 16 + 16)
                    dve.wait_ge(rows_in, f_ * 16 + 16)
                    dve.wait_ge(inv_ready[0], f_ + 1)
                for t in range(TT):
                    if part == 0:
                        nc.vector.scalar_tensor_tensor(out=x1[:, t, :], in0=xin[:, t, :], scalar=inv[:, 0, t:t + 1], in1=rows[:, 0, :],
                                                       op0=ALU.mult, op1=ALU.mult).then_inc(x1a, 1)
                    else:
                        dve.wait_ge(x1a, f_ * TT + t + 1)
                        nc.vector.tensor_tensor(x1[:, t, :], x1[:, t, :], rows[:, 1, :], ALU.add).then_inc(x1_ready, 1)

            def rope_tile(t):
                for m, name in enumerate("qk"):
                    n, c = body.turn("qkv", t, name)
                    dve.wait_ge(bank_filled[n], c)
                    q = bank[n][:, :].rearrange("p (h c j) -> p h c j", h=H, c=2)
                    r = rt[:, m, :, :].rearrange("p i (h c j) -> p i h c j", h=H, c=2)
                    tab = rope[:, t, :, :].rearrange("p a (o c j) -> p a o c j", o=1, c=2)
                    if t:
                        dve.wait_ge(rope_ready, f_ * 2 * TT + 2 * (t - 1) + m + 1)
                    nc.vector.tensor_tensor(rt[:, m, 0, :].rearrange("p (h j) -> p h j", h=H), bank[n][:, :].rearrange("p (h j) -> p h j", h=H),
                                            rope[:, t, 0:1, :].to_broadcast([P, H, HD]), ALU.mult)
                    for a in range(2):
                        ins = nc.vector.tensor_tensor(r[:, 1, :, a, :], q[:, :, 1 - a, :],
                                                      tab[:, 1, :, a, :].to_broadcast([P, H, HD // 2]), ALU.mult)
                    ins.then_inc(bank_free[n], 1)
                    dve.wait_ge(bank_free[n], c + 1)
                    nc.vector.tensor_tensor(rt[:, m, 0, :], rt[:, m, 0, :], rt[:, m, 1, :], ALU.add).then_inc(rope_sum, 1)
                n, c = body.turn("qkv", t, "v")
                dve.wait_ge(v_hi, f_ * TT + t + 1)
                nc.vector.tensor_tensor(v[:, t, :, HD:2 * HD], bank[n][:, :].rearrange("p (h d) -> p h d", h=H),
                                        v[:, t, :, 0:HD], ALU.subtract).then_inc(bank_free[n], 1)
                if t:
                    k_copy(t - 1)
                for m in range(2):
                    dve.wait_ge(rope_hi, f_ * 2 * TT + 2 * t + m + 1)
                    lo = 2 * HD if m == 0 else HD
                    nc.vector.tensor_tensor(stack[:, m, :, lo:lo + HD], rt[:, m, 0, :].rearrange("p (h j) -> p h j", h=H),
                                            stack[:, m, :, 0:HD], ALU.subtract).then_inc(rope_ready, 1)

            def head_max(h):
                for j in range(2):
                    dve.wait_ge(pair_filled[j], f_ * 2 * H + h + 1)
                    nc.vector.tensor_reduce(mx[:, h, 2 * j:2 * j + 2], pair[j][:, :, :], AX_X, ALU.max).then_inc(pair_free[j], 1)

            def negated_maxima():
                for j in range(2):
                    dve.wait_ge(pair_free[j], f_ * 2 * H + H + 1)
                nc.vector.tensor_scalar(nmf[:, :, :], mx[:, :, :].rearrange("p h t -> p t h"), -1.0, LN_SCALE * float(HD) ** 0.5,
                                        ALU.mult, ALU.add).then_inc(nm_step, 1)
                dve.wait_ge(nm_step, f_ * 2 + 1)
                nc.vector.tensor_copy(nm[:, :, :, 0], nmf[:, :, :]).then_inc(nm_step, 1)
                dve.wait_ge(nm_step, f_ * 2 + 2)
                nc.vector.tensor_tensor(nm[:, :, :, 1], nmf[:, :, :], nm[:, :, :, 0], ALU.subtract).then_inc(nm_ready, 1)

            def split_probs(h):
                for j in range(2):
                    if j == 0 and h >= 2:
                        dve.wait_ge(pv_filled, f_ * H + h - 1)
                    dve.wait_ge(pair_free[j], f_ * 2 * H + H + h + 2)
                    hi = front[:, h % 2, 0, j * 2 * S:(j + 1) * 2 * S]
                    lo = front[:, h % 2, 1, j * 2 * S:(j + 1) * 2 * S]
                    nc.vector.tensor_copy(hi, p32[:, j, :]).then_inc(p_hi, 1)
                    dve.wait_ge(p_hi, f_ * 2 * H + 2 * h + j + 1)
                    nc.vector.tensor_tensor(lo, p32[:, j, :], hi, ALU.subtract).then_inc(p_ready, 1)

            def add_pv(h):
                dve.wait_ge(o_copied, f_ * H + h + 1)
                nc.vector.tensor_tensor(osb[:, :, h, :], osb[:, :, h, :], pv[:, :, HD:2 * HD], ALU.add).then_inc(pv_free, 1)

            if b is not None:
                for k in range(KT):
                    n, c = body.turn("ot", k)
                    dve.wait_ge(ot_hi, b * KT + k + 1)
                    nc.vector.tensor_tensor(nxb[:, 1, k, :], bank[n][:, :], nxb[:, 0, k, :], ALU.subtract).then_inc(bank_free[n], 1)
                dve.wait_ge(stored, b * 16 * TT + 1)
                for t in range(TT):
                    add(("wo", t), t, x1)
                normalise(2, b, x2)
                norm_split(1, "n2", b)
                for f in range(FH):
                    gate_by_up(f)
                    if f:
                        h_low(f - 1)
                    if f_ is not None:
                        if f == 3:
                            modulate(0)
                        if f == 4:
                            modulate(1)
                        if f == 6:
                            normalise(1, f_, x1)
                h_low(FH - 1)
                add(("dn", 0, 0), 0, x2)
                add(("dn", 0, 1), 1, x2)
            elif f_ is not None:
                modulate(0)
                modulate(1)
                normalise(1, f_, x1)
            if f_ is not None:
                norm_split(0, "n1", f_)
            if b is not None:
                add(("dn", 0, 2), 2, x2)
                add(("dn", 0, 3), 3, x2)
            if f_ is not None:
                for t in range(TT):
                    rope_tile(t)
                k_copy(TT - 1)
            for h in range(H + 1):
                if f_ is not None and h < H:
                    head_max(h)
                if b is not None and h and h % 2 == 0:
                    f = FH + h // 2 - 1
                    gate_by_up(f)
                    if f > FH:
                        h_low(f - 1)
            if b is not None:
                h_low(FT - 1)
            if f_ is not None:
                negated_maxima()
            if b is not None:
                add(("dn", 1, 0), 0, x2)
            if f_ is not None:
                n, c = body.turn("mt")
                dve.wait_ge(bank_filled[n], c)
                nc.vector.tensor_copy(mrow[96:128, :], bank[n][:, :].bitcast(F16)[96:128, 0:S]).then_inc(bank_free[n], 1)
            if b is not None:
                add(("dn", 1, 1), 1, x2)
            for h in range(H):
                if f_ is not None:
                    split_probs(h)
                    if h:
                        add_pv(h - 1)
                if b is not None and h == 8:
                    add(("dn", 1, 2), 2, x2)
            if f_ is not None:
                add_pv(H - 1)
                nc.vector.reciprocal(rden[:, :, :], den[:, :, :]).then_inc(rden_ready, 1)
                dve.wait_ge(rden_ready, f_ + 1)
                dve.wait_ge(pv_free, f_ * H + H + 1)
                for t in range(TT):
                    nc.vector.tensor_tensor(osb[:, t, :, :], osb[:, t, :, :],
                                            rden[:, t, :].rearrange("p (h o) -> p h o", o=1).to_broadcast([P, H, HD]), ALU.mult).then_inc(o_ready, 1)
            if b is not None:
                add(("dn", 1, 3), 3, x2)

        bodies(dve, program)


def block_kernel(nc, w, out):
    with ExitStack() as ctx:
        def sb(name, shape, dt):
            return ctx.enter_context(nc.sbuf_tensor(name, shape, dt))

        def sem(name):
            return ctx.enter_context(nc.semaphore(name))

        res = {
            "wqkvo": sb("wqkvo", [P, 4, 2, KT, 512], F16),
            "wdn": sb("wdn", [P, 2, FT, 512], F16),
            "ident16": sb("ident16", [P, P], F16),
            "ident32": sb("ident32", [P, P], F32),
            "rope": sb("rope", [P, TT, 2, HD], F32),
            "kT": sb("kT", [P, H, S], F16),
            "v": sb("v", [P, TT, H, VW], F16),
            "brow": sb("brow", [P, 512], F16),
            "bones": sb("bones", [P, 4, P], F16),
            "bank_free": [sem(f"bank{k}_free") for k in range(RING)],
            "pair_free": [sem(f"pair{j}_free") for j in range(2)],
            "pv_free": sem("pv_free"), "stored": sem("stored"),
        }
        res["free"] = [*res["bank_free"], *res["pair_free"], res["pv_free"], res["stored"]]
        scratch = {
            "gu": nc.dram_tensor("gu_split", (FT, P, 2, 2, KT, P), F16).ap(),
            "rows": nc.dram_tensor("rows_all", (B, 1024), F32).ap(),
            "mods": nc.dram_tensor("mods_all", (B, P, 4 * KT), F32).ap(),
        }
        with ExitStack() as inner:
            prepare(nc, inner, w, res, scratch)
        with ExitStack() as inner:
            sequences(nc, inner, w, res, scratch, out)


_INS = {
    "x": "x", "cond_1024": "cond", "L0_cond_w_proj": "w_proj", "L0_cond_b_proj": "b_proj", "L0_cond_rms_weight": "rms_weight",
    "L1_cond_t1_w1": "t1_w1", "L1_cond_t1_w2": "t1_w2", "L1_cond_t2_w1": "t2_w1", "L1_cond_t2_w2": "t2_w2",
    "L1_cond_wq": "wq", "L1_cond_bq": "bq", "L1_cond_wk": "wk", "L1_cond_bk": "bk", "L1_cond_wv": "wv", "L1_cond_bv": "bv",
    "L1_cond_wo": "wo", "L1_cond_bo": "bo", "L1_cond_w_gate": "w_gate", "L1_cond_w_up": "w_up", "L1_cond_w_down": "w_down",
}


def _constants():
    import numpy as np
    freq = (np.float32(1.0) / np.float32(10000.0) ** (np.arange(0, 32, 2, dtype=np.float32) / np.float32(32))).astype(np.float32)
    angle = np.arange(512, dtype=np.float32)[:, None] * freq[None, :]
    c, s = np.cos(angle), np.sin(angle)
    rope = np.stack([np.concatenate([c, c], 1), np.concatenate([-s, s], 1)], 1).astype(np.float32) / np.float32(256)
    pick = (np.arange(32)[:, None] // 2 == np.arange(16)[None, :]).astype(np.float16)
    bones = np.zeros((128, 4, 128), np.float16)
    for m in range(4):
        bones[[m, 4 + m], m, :] = 1 if m < 3 else 256
    return {"bones": bones, "ident16": np.eye(128, dtype=np.float16), "ident32": np.eye(128, dtype=np.float32), "rope": rope, "pick": pick}


def _by_features(inputs):
    import numpy as np
    cols = lambda name: np.asarray(inputs["L1_cond_" + name]).reshape(-1, 128).T
    vecs = [np.concatenate([cols(f"t{i}_b1"), cols(f"t{i}_b2"), cols(f"w_norm{i}")], 1) for i in (1, 2)]
    cond_t = np.asarray(inputs["cond_1024"]).T.reshape(4, 128, 8).transpose(1, 0, 2)
    return {"vecs": np.stack(vecs, 1), "cond_t": cond_t}


def kernel(**inputs):
    import numpy as _np
    import concourse.bacc as _bacc
    from concourse import mybir as _mybir
    from concourse.bass_utils import run_bass_kernel_spmd as _run

    nc = _bacc.Bacc("TRN2", target_bir_lowering=False, num_devices=1)
    arrays, aps = {}, {}
    named = [(_INS[k], inputs[k]) for k in _INS] + list(_constants().items()) + list(_by_features(inputs).items())
    for name, value in named:
        a = _np.ascontiguousarray(value)
        arrays[f"in_{name}_dram"] = a
        aps[name] = nc.dram_tensor(f"in_{name}_dram", a.shape, _mybir.dt.from_np(a.dtype), kind="ExternalInput").ap()
    out = nc.dram_tensor("out_0_dram", (8, 512, 512), _mybir.dt.float32, kind="ExternalOutput").ap()
    block_kernel(nc, aps, out)
    r = _run(nc, [arrays], core_ids=[0])
    return r.results[0]["out_0_dram"]
```

```python
from contextlib import ExitStack

import concourse.bass as bass
from concourse import mybir

ALU = mybir.AluOpType
ACT = mybir.ActivationFunctionType
F32 = mybir.dt.float32
F16 = mybir.dt.float16
AX_X = mybir.AxisListType.X

P = 128
B, S, D = 8, 512, 512
H, HD = 16, 32
F = 2048
TT = S // P
KT = D // P
FT = F // P
FA = 5
FB = FT - FA
W_SCALE = 256.0
SQRT_D = float(D) ** 0.5
UNSCALE = 1.0 / W_SCALE
LN_SCALE = 8 * 0.6931471805599453
RING = 3
WRING = 2
VW = 2 * HD + 1


def bank_turns(pre, front, back):
    def qkv(t):
        return [("qkv", t, m) for m in "qkv"] if front else []

    def if_back(steps):
        return steps if back else []

    steps = qkv(1) + if_back([("wo", t) for t in range(TT)]) + qkv(2) + qkv(3)
    steps += if_back([(p, f) for f in range(FA) for p in "gu"] + [("dn", 0, 0), ("dn", 0, 1)])
    if pre:
        steps += [("n1", 0), ("n1", 1)]
    steps += if_back([("dn", 0, 2)])
    if pre:
        steps += [("n1", 2), ("n1", 3)]
    steps += if_back([("dn", 0, 3)] + [(p, f) for f in range(FA, FT) for p in "gu"] + [("dn", 1, 0)])
    if front:
        steps += [("mt",)]
    steps += if_back([("dn", 1, t) for t in range(1, TT)])
    if pre:
        steps += [("qkv", 0, m) for m in "qkv"]
    return {step: n for n, step in enumerate(steps)}


def pair_turns(front, back):
    if_front, if_back = (lambda steps: steps if front else []), (lambda steps: steps if back else [])
    steps = if_back([("ot",)]) + if_front([("st", 0), ("st", 1)]) + if_back([("n2", 0), ("n2", 1)])
    steps += if_front([("st", 2), ("st", 3)] + [("max", h) for h in range(H)] + [("probs", h) for h in range(H)])
    return {step: n for n, step in enumerate(steps)}


class Body:
    def __init__(self, before=(), it=None, pre=None, front=None, back=None):
        self.pre, self.front, self.back = pre, front, back
        self.turns = bank_turns(*(s is not None for s in (pre, front, back)))
        self.pair_turns = pair_turns(front is not None, back is not None)
        self.before, self.it = before, it
        self.starting = front is None and pre is not None
        self.filling = back is None and front is not None

    @staticmethod
    def count(turns, k):
        return len(range(k, len(turns), RING))

    def turn(self, *step):
        n = self.turns[step]
        k = n % RING
        before = sum(Body.count(body.turns, k) for body in self.before)
        if self.it is not None:
            before = self.it * Body.count(self.turns, k) + before
        return k, before + n // RING + 1

    def pair(self, *step):
        before = sum(len(body.pair_turns) for body in self.before)
        if self.it is not None:
            before = self.it * len(self.pair_turns) + before
        return before + self.pair_turns[step] + 1


def shared(n, h, heads=H):
    return range(min(n, h * n // heads), min(n, (h + 1) * n // heads))


def last_head(step, n, heads=H):
    return next(h for h in range(H) if step in shared(n, h, heads))


def bodies(engine, program):
    start = Body(pre=0)
    program(start)
    first = Body([start], pre=1, front=0)
    program(first)
    before = [start, first]
    with engine.Fori(0, B - 2) as it:
        loop = Body(before, it, pre=it + 2, front=it + 1, back=it)
        program(loop)
    before = before + [loop] * (B - 2)
    last_front = Body(before, front=B - 1, back=B - 2)
    program(last_front)
    program(Body(before + [last_front], back=B - 1))


class Residual:
    def __init__(self, nc, sb, sem):
        self.nc = nc
        self.xin = sb("xin", [P, TT, D], F32)
        self.p32 = sb("p32", [P, 2, 2 * S], F32)
        self.rows = self.p32[:, 0, :].rearrange("p (c d) -> p c d", c=2)
        self.junk = self.p32[:, 1, 0:D]
        self.mods = sb("mods", [P, 2, 2, KT], F32)
        self.mods_in = [sem("mods1_in"), sem("mods2_in")]
        self.ssq = sb("ssq", [P, 3, TT], F32)
        self.inv = sb("inv", [P, 3, TT], F32)
        self.half = sb("half", [P, TT], F32)
        self.eps_d = sb("eps_d", [P, 2, TT], F32)
        self.x_in, self.rows_in, self.half_set = sem("x_in"), sem("rows_in"), sem("half_set")
        self.sq, self.inv_pre, self.inv_ready = ([sem(f"{s}{i}") for i in range(3)] for s in ("sq", "inv_pre", "inv_ready"))
        self.x1a, self.x1_ready, self.x1_saved = sem("x1a"), sem("x1_ready"), sem("x1_saved")
        self.xn_ready = [sem("xn_ready0"), sem("xn_ready1")]

    def constants(self, pool):
        nc = self.nc
        nc.gpsimd.memset(self.half[:, :], -0.5).then_inc(self.half_set, 1)
        nc.gpsimd.memset(self.eps_d[:, 0, :], 1e-6 * D).then_inc(self.half_set, 1)
        nc.gpsimd.memset(self.eps_d[:, 1, :], 1e-5 * D).then_inc(self.half_set, 1)
        pool.wait_ge(self.half_set, 3)

    def load_tokens(self, pool, w, scratch, seq, first):
        pool.dma_start(self.xin[:, :, :], w["x"][seq].rearrange("(t p) d -> p t d", p=P)).then_inc(self.x_in, 16)
        if not first:
            self.load_rows(pool, scratch["rows"][bass.ds(seq, 1), :])

    def load_mods(self, pool, scratch, i, seq):
        pool.dma_start(self.mods[:, i, :, :].rearrange("p a k -> p (a k)"),
                       scratch["mods"][seq][:, i * 2 * KT:(i + 1) * 2 * KT]).then_inc(self.mods_in[i], 16)

    def load_rows(self, pool, src):
        pool.dma_start(self.rows.rearrange("p c d -> p (c d)"), src.to_broadcast([P, 2 * D])).then_inc(self.rows_in, 16)

    def squares(self, act, i, seq, src, ready):
        for t in range(TT):
            ready(t)
            self.nc.scalar.activation(self.junk, src[:, t, :], ACT.Square, accum_out=self.ssq[:, i, t:t + 1]).then_inc(self.sq[i], 1)
            act.wait_ge(self.sq[i], seq * TT + t + 1)

    def inverse(self, pool, i, seq):
        ssq = self.ssq[:, i, :]
        pool.wait_ge(self.sq[i], seq * TT + TT)
        self.nc.gpsimd.tensor_tensor(ssq, ssq, self.eps_d[:, min(i, 1), :], ALU.add).then_inc(self.inv_pre[i], 1)
        pool.wait_ge(self.inv_pre[i], seq + 1)
        self.nc.gpsimd.tensor_tensor(self.inv[:, i, :], ssq, self.half[:, :], ALU.pow).then_inc(self.inv_ready[i], 1)

    def modulate(self, dve, seq, part):
        xin, rows = self.xin, self.rows
        if part == 0:
            dve.wait_ge(self.x_in, seq * 16 + 16)
            dve.wait_ge(self.rows_in, seq * 16 + 16)
            dve.wait_ge(self.inv_ready[0], seq + 1)
        for t in range(TT):
            if part == 0:
                self.nc.vector.scalar_tensor_tensor(out=xin[:, t, :], in0=xin[:, t, :], scalar=self.inv[:, 0, t:t + 1], in1=rows[:, 0, :],
                                                    op0=ALU.mult, op1=ALU.mult).then_inc(self.x1a, 1)
            else:
                dve.wait_ge(self.x1a, seq * TT + t + 1)
                self.nc.vector.tensor_tensor(xin[:, t, :], xin[:, t, :], rows[:, 1, :], ALU.add).then_inc(self.x1_ready, 1)

    def keep_x1(self, sp, scratch, seq):
        sp.wait_ge(self.x1_ready, seq * TT + TT)
        sp.dma_start(scratch["x1"][seq], self.xin[:, :, :]).then_inc(self.x1_saved, 16)

    def normalise(self, act, i, seq, src):
        act.wait_ge(self.inv_ready[i], seq + 1)
        if i == 1:
            act.wait_ge(self.x1_saved, seq * 16 + 16)
        for t in range(TT):
            self.nc.scalar.activation(self.xin[:, t, :], src[:, t, :], ACT.Copy, scale=self.inv[:, i, t:t + 1]).then_inc(self.xn_ready[i - 1], 1)

    def first_squares(self, act, seq):
        self.squares(act, 0, seq, self.xin, lambda t: act.wait_ge(self.x_in, seq * 16 + 16))

    def second_squares(self, act, seq):
        self.squares(act, 1, seq, self.xin, lambda t: act.wait_ge(self.x1_ready, seq * TT + t + 1))


def prepare(nc, ctx, w, res, scratch):
    def sb(name, shape, dt=F32):
        return ctx.enter_context(nc.sbuf_tensor(name, shape, dt))

    def sem(name):
        return ctx.enter_context(nc.semaphore(name))

    stage = res["wdn"][:, :, :, :].rearrange("p i f n -> p (i f n)").bitcast(F32).rearrange("p (m k n) -> p m k n", m=4, k=KT)
    cond = sb("p_cond", [B, D])
    cond_t = sb("p_cond_t", [P, KT, B])
    wp = sb("p_wp", [P, 8, 512])
    tern = sb("p_tern", [P, 8, 512], F16)
    tern_t = sb("p_tern_t", [P, KT, 1024], F16)
    pick = sb("p_pick", [P, H], F16)
    absum = sb("p_absum", [P, 1])
    mean = sb("p_mean", [P, 1])
    wscale = sb("p_wscale", [P, 1])
    cmax = sb("p_cmax", [B, 1])
    cinv = sb("p_cinv", [B, 1])
    cfac = sb("p_cfac", [B, 1])
    cint = cond
    cint16 = sb("p_cint16", [B, D], F16)
    cint_t = sb("p_cint_t", [P, KT, B], F16)
    bproj = sb("p_bproj", [B, 1024])
    rmsw = sb("p_rmsw", [B, D])
    emb = sb("p_emb", [B, 1024])
    ones = sb("p_ones", [P, P])
    w1 = sb("p_w1", [P, 2, KT, 512])
    w2 = sb("p_w2", [P, 2, KT, 1024])
    vecs = sb("p_vecs", [P, 2, 4 * KT])
    b1, b2, wn = vecs[:, :, 0:KT], vecs[:, :, KT:3 * KT], vecs[:, :, 3 * KT:4 * KT]
    z = sb("p_z", [P, KT, B])
    ez = sb("p_ez", [P, KT, B])
    y = sb("p_y", [P, 8, B])
    mods = sb("p_mods", [P, 2, B, 2, KT])
    bias4 = sb("p_bias4", [4, 512])
    bsplit = sb("p_bsplit", [4, 2, 512], F16)

    ps_t = ctx.enter_context(nc.psum_tensor("p_ps_t", [P, 2, 1024], F16))
    ps_e = ctx.enter_context(nc.psum_tensor("p_ps_e", [P, 2, 512], F32))
    ps_s = ctx.enter_context(nc.psum_tensor("p_ps_s", [P, 512], F32))
    ps_m = ctx.enter_context(nc.psum_tensor("p_ps_m", [P, 512], F32))

    staged = [sem(f"p_staged{m}") for m in range(4)]
    hi_done, lo_done = sem("p_hi_done"), sem("p_lo_done")
    small, wp_in, w12_in = sem("p_small"), sem("p_wp_in"), [sem("p_w12_in0"), sem("p_w12_in1")]
    consts_in = sem("p_consts_in")
    v = sem("p_vector_step")
    abs_done, tr_done, tr_free = sem("p_abs_done"), sem("p_tr_done"), sem("p_tr_free")
    sum_done, emb_done, emb_out = sem("p_sum_done"), sem("p_emb_done"), sem("p_emb_out")
    ones_set, sil_inv = sem("p_ones_set"), sem("p_silu_inv")
    mlp1, mlp2, sil = sem("p_mlp1"), sem("p_mlp2"), sem("p_silu")
    z_ready, h_ready, y_used = sem("p_z_ready"), sem("p_h_ready"), sem("p_y_used")
    mods_ready, mods_out = sem("p_mods_ready"), [sem("p_mods_out0"), sem("p_mods_out1")]
    pick_in, ident_in = sem("p_pick_in"), sem("p_ident_in")
    bias_in, bias_hi, brow_in = sem("p_bias_in"), sem("p_bias_hi"), sem("p_brow_in")

    rs = res["residual"]

    block = ctx.enter_context(nc.Block())

    @block.sync
    def _(sp):
        sp.dma_start(res["ident16"][:, :], w["ident16"]).then_inc(ident_in, 16)
        sp.dma_start(pick[96:128, :], w["pick"]).then_inc(pick_in, 16)

        def layers(i):
            sp.dma_start(w1[:, i, :, :], w[f"t{i+1}_w1"].rearrange("(k p) n -> p k n", p=P)).then_inc(w12_in[i], 16)
            sp.dma_start(w2[:, i, :, :], w[f"t{i+1}_w2"].rearrange("(k p) n -> p k n", p=P)).then_inc(w12_in[i], 16)

        layers(0)
        layers(1)
        sp.dma_start(res["ident32"][:, :], w["ident32"]).then_inc(consts_in, 16)
        sp.dma_start(res["rope"][:, :, :, :], w["rope"].rearrange("(t p) c j -> p t c j", p=P)).then_inc(consts_in, 16)
        sp.dma_start(res["bones"][:, :, :], w["bones"]).then_inc(consts_in, 16)
        sp.wait_ge(w12_in[1], 32)
        for m, name in enumerate(["wq", "wk", "wv", "wo"]):
            sp.dma_start(stage[:, m, :, :], w[name].rearrange("(k p) n -> p k n", p=P)).then_inc(staged[m], 16)
        for i in range(2):
            if i == 1:
                rs.keep_x1(sp, scratch, 0)
            sp.wait_ge(mods_ready, 2 * i + 2)
            sp.dma_start(scratch["mods"][:, :, i * 2 * KT:(i + 1) * 2 * KT].rearrange("b p c -> p b c"),
                         mods[:, i, :, :, :].rearrange("p b a k -> p b (a k)")).then_inc(mods_out[i], 16)
        sp.wait_ge(mods_out[1], 16)
        sp.wait_ge(rs.x1_saved, 16)
        sp.wait_ge(consts_in, 48)

    @block.gpsimd
    def _(pool):
        nc.gpsimd.memset(ones[:, :], 1.0).then_inc(ones_set, 1)
        pool.dma_start(wp[:, :, :], w["w_proj"].rearrange("(r p) c -> p r c", p=P)).then_inc(wp_in, 16)
        rs.load_tokens(pool, w, scratch, 0, first=True)
        rs.constants(pool)
        rs.inverse(pool, 0, 0)
        pool.wait_ge(v, 13)
        for i in range(2):
            pool.dma_start(res["brow"][4 * i:4 * i + 4, :], bsplit[:, i, :]).then_inc(brow_in, 16)
        pool.wait_ge(v, 17)
        pool.dma_start(scratch["rows"], emb[:, :]).then_inc(emb_out, 16)
        pool.wait_ge(emb_out, 16)
        rs.load_rows(pool, scratch["rows"][0:1, :])
        pool.wait_ge(mods_out[0], 16)
        rs.load_mods(pool, scratch, 0, 0)
        pool.wait_ge(brow_in, 32)
        rs.inverse(pool, 1, 0)

    @block.scalar
    def _(act):
        act.dma_start(cond[:, :], w["cond"]).then_inc(small, 16)
        act.dma_start(bproj[:, :], w["b_proj"].rearrange("(o n) -> o n", o=1).to_broadcast([B, 1024])).then_inc(small, 16)
        act.dma_start(rmsw[:, :], w["rms_weight"].rearrange("(o n) -> o n", o=1).to_broadcast([B, D])).then_inc(small, 16)
        act.dma_start(cond_t[:, :, :], w["cond_t"]).then_inc(small, 16)
        act.dma_start(vecs[:, :, :], w["vecs"]).then_inc(small, 16)
        for m, name in enumerate(["bq", "bk", "bv", "bo"]):
            act.dma_start(bias4[m:m + 1, :], w[name].rearrange("(o n) -> o n", o=1)).then_inc(bias_in, 16)
        act.wait_ge(wp_in, 16)
        nc.scalar.activation(tern[:, :, :], wp[:, :, :], ACT.Abs, accum_out=absum[:, :]).then_inc(abs_done, 1)
        def exponential(i):
            act.wait_ge(z_ready, i + 1)
            nc.scalar.activation(ez[:, :, :], z[:, :, :], ACT.Exp, scale=-1.0).then_inc(sil, 1)

        def high(m):
            act.wait_ge(staged[m], 16)
            nc.scalar.activation(res["wqkvo"][:, m, 0, :, :], stage[:, m, :, :], ACT.Copy, scale=W_SCALE).then_inc(hi_done, 1)

        exponential(0)
        rs.first_squares(act, 0)
        for m in range(4):
            high(m)
        exponential(1)
        rs.second_squares(act, 0)
        rs.normalise(act, 1, 0, rs.xin)

    @block.tensor
    def _(pe):
        pe.wait_ge(ident_in, 16)
        pe.wait_ge(ones_set, 1)
        pe.wait_ge(abs_done, 1)
        nc.tensor.matmul(ps_s[:, 0:1], ones[:, :], absum[:, :], start=True, stop=True).then_inc(sum_done, 1)
        def first_layer(i):
            pe.wait_ge(small, 16 * 5)
            pe.wait_ge(w12_in[i], 32)
            if i:
                pe.wait_ge(y_used, 1)
            for m in range(KT):
                for k in range(KT):
                    mm = nc.tensor.matmul(ps_m[:, m * B:(m + 1) * B], w1[:, i, k, m * P:(m + 1) * P], cond_t[:, k, :],
                                          start=(k == 0), stop=(k == KT - 1))
            mm.then_inc(mlp1, 1)

        def second_layer(i):
            pe.wait_ge(h_ready, i + 1)
            for m in range(8):
                for k in range(KT):
                    mm = nc.tensor.matmul(ps_m[:, 64 + m * B:64 + (m + 1) * B], w2[:, i, k, m * P:(m + 1) * P], z[:, k, :],
                                          start=(k == 0), stop=(k == KT - 1))
            mm.then_inc(mlp2, 1)

        first_layer(0)
        pe.wait_ge(v, 6)
        for k in range(KT):
            if k >= 2:
                pe.wait_ge(tr_free, k - 1)
            for r in range(8):
                mm = nc.tensor.transpose(ps_t[:, k % 2, r * P:(r + 1) * P], tern[:, r, k * P:(k + 1) * P], res["ident16"][:, :])
            mm.then_inc(tr_done, 1)
        pe.wait_ge(v, 10)
        pe.wait_ge(tr_free, 3)
        for k in range(KT):
            mm = nc.tensor.transpose(ps_t[:, 0, k * B:(k + 1) * B], cint16[:, k * P:(k + 1) * P], res["ident16"][0:B, 0:B])
        mm.then_inc(tr_done, 1)
        pe.wait_ge(tr_free, 5)
        for c in range(2):
            for k in range(KT):
                mm = nc.tensor.matmul(ps_e[0:B, c, :], cint_t[:, k, :], tern_t[:, k, c * 512:(c + 1) * 512],
                                      start=(k == 0), stop=(k == KT - 1))
        mm.then_inc(emb_done, 1)
        second_layer(0)
        first_layer(1)
        second_layer(1)

    @block.vector
    def _(dve):
        n_step = [0]

        def then(ins):
            n_step[0] += 1
            ins.then_inc(v, 1)
            dve.wait_ge(v, n_step[0])

        def split_lo(m):
            dve.wait_ge(hi_done, m + 1)
            nc.vector.scalar_tensor_tensor(out=res["wqkvo"][:, m, 1, :, :], in0=stage[:, m, :, :], scalar=W_SCALE,
                                           in1=res["wqkvo"][:, m, 0, :, :], op0=ALU.mult, op1=ALU.subtract).then_inc(lo_done, 1)

        def hidden(i):
            dve.wait_ge(mlp1, i + 1)
            nc.vector.tensor_tensor(z[:, :, :], ps_m[:, 0:KT * B].rearrange("p (k b) -> p k b", b=B),
                                    b1[:, i, :].rearrange("p (k o) -> p k o", o=1).to_broadcast([P, KT, B]), ALU.add).then_inc(z_ready, 1)

        def silu(i):
            dve.wait_ge(sil, i + 1)
            nc.vector.tensor_scalar(ez[:, :, :], ez[:, :, :], 1.0, None, ALU.add).then_inc(mods_ready, 1)
            dve.wait_ge(mods_ready, 2 * i + 1)
            nc.vector.reciprocal(ez[:, :, :], ez[:, :, :]).then_inc(sil_inv, 1)
            dve.wait_ge(sil_inv, i + 1)
            dve.wait_ge(z_ready, i + 1)
            nc.vector.tensor_tensor(z[:, :, :], z[:, :, :], ez[:, :, :], ALU.mult).then_inc(h_ready, 1)

        def modulations(i):
            dve.wait_ge(mlp2, i + 1)
            nc.vector.tensor_tensor(y[:, :, :], ps_m[:, 64:64 + 8 * B].rearrange("p (k b) -> p k b", b=B),
                                    b2[:, i, :].rearrange("p (k o) -> p k o", o=1).to_broadcast([P, 8, B]), ALU.add).then_inc(y_used, 1)
            dve.wait_ge(y_used, 2 * i + 1)
            nc.vector.tensor_scalar(y[:, 0:KT, :], y[:, 0:KT, :], 1.0, SQRT_D, ALU.add, ALU.mult).then_inc(y_used, 1)
            dve.wait_ge(y_used, 2 * i + 2)
            wnb = wn[:, i, :].rearrange("p (k o) -> p k o", o=1).to_broadcast([P, KT, B])
            nc.vector.tensor_tensor(mods[:, i, :, 0, :].rearrange("p b k -> p k b"), y[:, 0:KT, :], wnb, ALU.mult)
            nc.vector.tensor_copy(mods[:, i, :, 1, :].rearrange("p b k -> p k b"), y[:, KT:8, :]).then_inc(mods_ready, 1)

        nc.vector.memset(res["brow"][:, :], 0.0)
        then(nc.vector.memset(res["v"][:, :, :, 2 * HD:VW], 1.0))
        dve.wait_ge(pick_in, 16)
        then(nc.vector.tensor_copy(res["kT"][96:128, :, :], pick[96:128, :].rearrange("p (h o) -> p h o", o=1).to_broadcast([32, H, S])))
        magic = 12582912.0
        dve.wait_ge(sum_done, 1)
        then(nc.vector.tensor_scalar(mean[:, :], ps_s[:, 0:1], 1.0 / (1024 * 512), 1e-5, ALU.mult, ALU.max))
        then(nc.vector.reciprocal(wscale[:, :], mean[:, :]))
        then(nc.vector.tensor_scalar(wp[:, :, :], wp[:, :, :], wscale[:, 0:1], magic, ALU.mult, ALU.add))
        dve.wait_ge(small, 16 * 5)
        hidden(0)
        nc.vector.tensor_scalar(wp[:, :, :], wp[:, :, :], -magic, -1.0, ALU.add, ALU.max).then_inc(bias_hi, 1)
        silu(0)
        dve.wait_ge(bias_hi, 1)
        then(nc.vector.tensor_scalar(tern[:, :, :], wp[:, :, :], 1.0, None, ALU.min))
        then(nc.vector.tensor_reduce(cmax[:, :], cond[:, :], AX_X, ALU.max, apply_absolute_value=True))
        nc.vector.tensor_scalar(cmax[:, :], cmax[:, :], 1e-5, None, ALU.max).then_inc(bias_hi, 1)
        dve.wait_ge(bias_hi, 2)
        then(nc.vector.reciprocal(cinv[:, :], cmax[:, :]))
        nc.vector.tensor_scalar(cinv[:, :], cinv[:, :], 127.0, None, ALU.mult).then_inc(bias_hi, 1)
        dve.wait_ge(bias_hi, 3)
        then(nc.vector.tensor_scalar(cint[:, :], cond[:, :], cinv[:, 0:1], magic, ALU.mult, ALU.add))
        nc.vector.tensor_scalar(cint[:, :], cint[:, :], -magic, -128.0, ALU.add, ALU.max).then_inc(bias_hi, 1)
        dve.wait_ge(bias_hi, 4)
        then(nc.vector.tensor_scalar(cint16[:, :], cint[:, :], 127.0, None, ALU.min))
        then(nc.vector.tensor_scalar(cfac[:, :], cmax[:, :], 1.0 / 127.0, mean[0:B, 0:1], ALU.mult, ALU.mult))
        for k in range(KT):
            dve.wait_ge(tr_done, k + 1)
            nc.vector.tensor_copy(tern_t[:, k, :], ps_t[:, k % 2, :]).then_inc(tr_free, 1)
        dve.wait_ge(tr_done, 5)
        nc.vector.tensor_copy(cint_t[:, :, :], ps_t[:, 0, 0:KT * B].rearrange("p (k b) -> p k b", b=B)).then_inc(tr_free, 1)
        dve.wait_ge(bias_in, 16 * 4)
        then(nc.vector.tensor_scalar(bsplit[:, 0, :], bias4[:, :], W_SCALE, None, ALU.mult))
        then(nc.vector.scalar_tensor_tensor(out=bsplit[:, 1, :], in0=bias4[:, :], scalar=W_SCALE,
                                            in1=bsplit[:, 0, :], op0=ALU.mult, op1=ALU.subtract))
        dve.wait_ge(emb_done, 1)
        for c in range(2):
            nc.vector.scalar_tensor_tensor(out=emb[:, c * 512:(c + 1) * 512], in0=ps_e[0:B, c, :], scalar=cfac[:, 0:1],
                                           in1=bproj[:, c * 512:(c + 1) * 512], op0=ALU.mult, op1=ALU.add).then_inc(v, 1)
        dve.wait_ge(v, 15)
        nc.vector.scalar_tensor_tensor(out=emb[:, 0:D], in0=emb[:, 0:D], scalar=1.0, in1=rmsw[:, :],
                                       op0=ALU.add, op1=ALU.mult).then_inc(v, 1)
        dve.wait_ge(v, 16)
        nc.vector.tensor_scalar(emb[:, 0:D], emb[:, 0:D], SQRT_D, None, ALU.mult).then_inc(v, 1)
        split_lo(0)
        modulations(0)
        split_lo(1)
        rs.modulate(dve, 0, 0)
        hidden(1)
        silu(1)
        rs.modulate(dve, 0, 1)
        split_lo(2)
        split_lo(3)
        modulations(1)
        for s in res["free"]:
            dve.sem_inc(s, 1)


def sequences(nc, ctx, w, res, scratch, out):
    def sb(name, shape, dt=F32):
        return ctx.enter_context(nc.sbuf_tensor(name, shape, dt))

    def sem(name):
        return ctx.enter_context(nc.semaphore(name))

    wq, wdn, ident16, ident32 = res["wqkvo"], res["wdn"], res["ident16"], res["ident32"]
    rope, kT, v, brow, bones = res["rope"], res["kT"], res["v"], res["brow"], res["bones"]
    bank_free, pair_free, pv_free, stored = res["bank_free"], res["pair_free"], res["pv_free"], res["stored"]

    steps = res["residual"]
    xin, p32, xn_ready = steps.xin, steps.p32, steps.xn_ready
    osb = xin[:, :, :].rearrange("p t (h d) -> p t h d", h=H)
    x2 = sb("x2", [P, TT, D])
    mods = steps.mods
    nxa = sb("nxa", [P, 2, KT, S], F16)
    nxb = sb("nxb", [P, 2, KT, S], F16)
    qT = sb("qT", [P, H, S], F16)
    wgu = sb("wgu", [P, WRING, 2, 2, KT, P], F16)
    acts = sb("acts", [P, 2, 512])
    hf = sb("hf", [P, 2, 512])
    hT = sb("hT", [P, 2, FB, S], F16)
    den = sb("den", [P, TT, H])
    rden = sb("rden", [P, TT, H])
    front = sb("front", [P, 2, 2, TT * S], F16)
    front_flat = front[:, :, :, :].rearrange("p a b n -> p (a b n)")
    rt = front_flat[:, 0:4096].bitcast(F32).rearrange("p (m i n) -> p m i n", m=2, i=2)
    stack = front_flat[:, 4096:4096 + 2 * H * 96].rearrange("p (m h c) -> p m h c", m=2, h=H)
    mx = sb("mx", [P, H, TT])
    nmf = sb("nmf", [P, TT, H])
    nm = sb("nm", [P, TT, H, 2], F16)
    mrow = sb("mrow", [P, S], F16)

    pair = [ctx.enter_context(nc.psum_tensor(f"pair{j}", [P, 2, 512], F32)) for j in range(2)]
    pvb = ctx.enter_context(nc.psum_tensor("pvb", [P, 512], F32))
    bank = [ctx.enter_context(nc.psum_tensor(f"bank{k}", [P, 512], F32)) for k in range(RING)]
    pv = pvb[:, 0:TT * VW].rearrange("p (t c) -> p t c", t=TT)

    hT_flat = hT[:, :, :, :].rearrange("p i f s -> p (i f s)")
    stage = [wgu[:, :, :, :, :, :].rearrange("p s g i k n -> p (s g i k n)").bitcast(F32), hT_flat[:, 0:4096].bitcast(F32)]
    parts_out = [hT_flat[:, 4096:8192].rearrange("p (i n) -> p i n", i=2), nxb[:, :, :, :].rearrange("p i k n -> p i (k n)")]
    units = [("gu", g, k) for g in range(2) for k in range(KT)] + [("dn", 0, c) for c in range(FT // 4)]
    N_GU = 2 * KT
    UNITS_AHEAD = [0, 1]
    UNITS_TOKENS = {t: t + 1 for t in range(1, TT)}
    UNITS_MAX = {2 + 3 * i: 5 + i for i in range(4)}
    UNITS_BETWEEN = [9, 10]
    UNITS_PROBS = {1: 11}

    def unit_parts(n):
        kind, _, c = units[n]
        if kind == "dn":
            return [wdn[:, i, 4 * c:4 * c + 4, :] for i in range(2)], stage[n % 2].rearrange("p (f n) -> p f n", f=4)
        return [parts_out[n % 2][:, i, :] for i in range(2)], stage[n % 2]

    bank_filled = [sem(f"bank{k}_filled") for k in range(RING)]
    pair_filled = [sem(f"pair{j}_filled") for j in range(2)]
    pv_filled = sem("pv_filled")
    mods_in = steps.mods_in
    wgu_in = [sem(f"wgu_in{i}") for i in range(WRING)]
    staged, kept = ([sem(f"{s}{i}") for i in range(2)] for s in ("staged", "kept"))
    unit_hi, unit_lo = sem("unit_hi"), sem("unit_lo")
    x1_in = sem("x1_in")
    nx_ready = [sem("nx_ready0"), sem("nx_ready1")]
    rope_sum, rope_hi, rope_ready = sem("rope_sum"), sem("rope_hi"), sem("rope_ready")
    v_hi = sem("v_hi")
    nm_step, nm_ready = sem("nm_step"), sem("nm_ready")
    mrow_in = sem("mrow_in")
    p_hi, p_ready = sem("p_hi"), sem("p_ready")
    o_copied, rden_ready, o_ready = sem("o_copied"), sem("rden_ready"), sem("o_ready")
    ot_hi = sem("ot_hi")
    h_hi, h_ready = sem("h_hi"), sem("h_ready")

    PARTS = [(0, 0), (0, 1), (1, 0)]
    INV_SQRT_HD = 1.0 / float(HD) ** 0.5
    nx = [nxa, nxb]
    BEFORE_TURN, AFTER_TURN = 4, 6
    AT_ONCE = 3
    REST = FB * TT - BEFORE_TURN - AFTER_TURN - AT_ONCE
    FIRST_NORM = (1, 4, 7, 11)


    def norm_tile(body, i, seq, k):
        if i == 0:
            n, c = body.turn("n1", k)
            return bank[n][:, :], bank_filled[n], bank_free[n], c
        j = k // 2
        return pair[j][:, k % 2, :], pair_filled[j], pair_free[j], body.pair("n2", k % 2)

    block = ctx.enter_context(nc.Block())

    @block.sync
    def _(sp):
        def program(body):
            n_, f_, b = body.pre, body.front, body.back

            def weights(f):
                n, c = body.turn("u", f)
                if f_ is None and f + WRING >= FT:
                    return
                sp.wait_ge(bank_filled[n], c)
                sp.dma_start(wgu[:, f % WRING, :, :, :, :], scratch["gu"][(f + WRING) % FT]).then_inc(wgu_in[f % WRING], 16)

            def store(t):
                n, c = body.turn("dn", 1, t)
                sp.wait_ge(bank_free[n], c + 1)
                sp.dma_start(out[b, t * P:(t + 1) * P, :], x2[:, t, :]).then_inc(stored, 16)

            def stage_unit(n):
                kind, g, c = units[n]
                name = ("w_gate", "w_up")[g] if kind == "gu" else "w_down"
                if kind == "gu":
                    src = w[name][c * P:(c + 1) * P, :]
                else:
                    src = w[name][c * 512:(c + 1) * 512, :].rearrange("(f p) n -> p f n", p=P)
                sp.dma_start(unit_parts(n)[1], src).then_inc(staged[n % 2], 16)

            def unit_done(n):
                sp.wait_ge(unit_lo, n + 1)
                kind, g, c = units[n]
                if kind == "gu":
                    for i in range(2):
                        dst = scratch["gu"][:, :, g, i, c, :].rearrange("f p n -> p f n")
                        sp.dma_start(dst, unit_parts(n)[0][i].rearrange("p (f n) -> p f n", f=FT)).then_inc(kept[n % 2], 16)
                if n + 2 < len(units):
                    stage_unit(n + 2)

            if b is not None:
                for f in range(FT):
                    if f == FA - 1 and n_ is not None:
                        steps.keep_x1(sp, scratch, n_)
                    weights(f)
            elif body.starting:
                stage_unit(0)
                stage_unit(1)
                for n in UNITS_AHEAD:
                    unit_done(n)
            elif body.filling:
                for n in [*UNITS_TOKENS.values(), *UNITS_MAX.values()]:
                    if n == UNITS_MAX[FIRST_NORM[1] + 1]:
                        steps.keep_x1(sp, scratch, n_)
                    unit_done(n)
            if f_ is not None:
                n, c = body.turn("mt")
                sp.wait_ge(bank_free[n], c + 1)
                sp.dma_start(qT[96:128, :, :], mrow[96:128, :].rearrange("p (o s) -> p o s", o=1).to_broadcast([32, H, S])).then_inc(mrow_in, 16)
            if b is not None:
                for t in range(TT):
                    store(t)
                if f_ is not None:
                    sp.wait_ge(stored, (b + 1) * 16 * TT + 1)
            if f_ is not None:
                sp.dma_start(x2[:, :, :], scratch["x1"][f_]).then_inc(x1_in, 16)
            if body.filling:
                for n in [*UNITS_BETWEEN, *UNITS_PROBS.values()]:
                    unit_done(n)
                for j in range(2):
                    sp.wait_ge(kept[j], 16 * N_GU)
                for f in range(WRING):
                    sp.dma_start(wgu[:, f, :, :, :, :], scratch["gu"][f]).then_inc(wgu_in[f], 16)

        bodies(sp, program)
        sp.wait_ge(stored, 16 * TT * B + 1)

    @block.gpsimd
    def _(pool):
        def program(body):
            n_, f_, b = body.pre, body.front, body.back
            if b is not None:
                steps.inverse(pool, 2, b)
                pool.wait_ge(nx_ready[1], b * KT + KT)
            elif f_ is not None:
                pool.wait_ge(nx_ready[0], f_ * KT + KT)
            if n_ is not None and not body.starting:
                steps.load_tokens(pool, w, scratch, n_, first=False)
            for i, seq in enumerate((n_, f_)):
                if seq is not None and not body.starting:
                    steps.load_mods(pool, scratch, i, seq)
            if n_ is not None and not body.starting:
                steps.inverse(pool, 0, n_)
                steps.inverse(pool, 1, n_)

        bodies(pool, program)

    @block.tensor
    def _(pe):
        def program(body):
            n_, f_, b = body.pre, body.front, body.back

            def norm_transposes(i, seq, tiles=range(KT)):
                for k in tiles:
                    ps, filled, free, c = norm_tile(body, i, seq, k)
                    if i == 0 or k % 2 == 0:
                        pe.wait_ge(free, c)
                    for t in range(TT):
                        if k == 0:
                            pe.wait_ge(xn_ready[i], seq * TT + t + 1)
                        mm = nc.tensor.transpose(ps[:, t * P:(t + 1) * P], xin[:, t, k * P:(k + 1) * P], ident32[:, :])
                    mm.then_inc(filled, 1)

            def project(step, lhs, rhs, steps, bias=None, wait=None, only=None):
                n, c = body.turn(*step)
                if only is None or only[0] == 0:
                    pe.wait_ge(bank_free[n], c)
                if bias is not None:
                    nc.tensor.matmul(bank[n][:, :], bones[:, bias, :], brow[:, :], start=True, stop=False)
                for k in range(steps) if only is None else range(*only):
                    if wait is not None:
                        wait(k)
                    for p, q in PARTS:
                        mm = nc.tensor.matmul(bank[n][:, :], lhs(p, k), rhs(q, k), start=(bias is None and k == 0 and p + q == 0),
                                              stop=(k == steps - 1 and (p, q) == PARTS[-1]))
                if only is None or only[1] == steps:
                    mm.then_inc(bank_filled[n], 1)

            def stack_transposes(t):
                for m in range(2):
                    pe.wait_ge(rope_ready, f_ * 2 * TT + 2 * t + m + 1)
                    pe.wait_ge(pair_free[m], body.pair("st", t))
                    for h in range(H):
                        mm = nc.tensor.transpose(pair[m][:, h // 8, :].bitcast(F16)[0:96, h % 8 * P:(h % 8 + 1) * P],
                                                 stack[:, m, h, :], ident16[:, :])
                    mm.then_inc(pair_filled[m], 1)

            def gate_or_up(f, u):
                i = f % WRING
                if not u:
                    pe.wait_ge(wgu_in[i], (b * (FT // WRING) + f // WRING + 1) * 16)
                project(("gu"[u], f), lambda p, k: wgu[:, i, u, p, k, :], lambda q, k: nxb[:, q, k, :], KT)

            def down(part, t, only=None):
                wait = None
                if t == 0:
                    wait = lambda f: pe.wait_ge(h_ready, b * FT + part * FA + f + 1)
                project(("dn", part, t), lambda p, f: hT[:, p, f, t * P:(t + 1) * P],
                        lambda q, f: wdn[:, q, part * FA + f, :], (FA, FB)[part], wait=wait, only=only)

            def down_steps(steps):
                for n in steps:
                    down(1, n // FB, only=(n % FB, n % FB + 1))

            def scores_by_queries(h):
                for j in range(2):
                    pe.wait_ge(pair_free[j], body.pair("max", h))
                    for i in range(2):
                        t = 2 * j + i
                        mm = nc.tensor.matmul(pair[j][:, i, :], qT[0:96, h, t * P:(t + 1) * P], kT[0:96, h, :], start=True, stop=True)
                    mm.then_inc(pair_filled[j], 1)

            def scores_by_keys(h):
                for j in range(2):
                    pe.wait_ge(pair_free[j], body.pair("probs", h))
                    for i in range(2):
                        t = 2 * j + i
                        mm = nc.tensor.matmul(pair[j][:, i, :], kT[:, h, t * P:(t + 1) * P], qT[:, h, :], start=True, stop=True)
                    mm.then_inc(pair_filled[j], 1)

            def probs_v(h):
                pe.wait_ge(p_ready, f_ * 2 * H + 2 * h + 2)
                pe.wait_ge(pv_free, f_ * H + h + 1)
                for s in range(TT):
                    for k in range(TT):
                        for a in range(2):
                            mm = nc.tensor.matmul(pvb[:, s * VW:(s + 1) * VW], front[:, h % 2, a, k * S + s * P:k * S + (s + 1) * P],
                                                  v[:, k, h, :], start=(k == 0 and a == 0), stop=(k == TT - 1 and a == 1))
                mm.then_inc(pv_filled, 1)

            def project_qkv(t, m):
                name = "qkv"[m]
                project(("qkv", t, name), lambda p, k: nxa[:, p, k, t * P:(t + 1) * P], lambda q, k: wq[:, m, q, k, :], KT, bias=m)

            def qkv(t):
                project_qkv(t, 0)
                project_qkv(t, 1)
                stack_transposes(t - 1)
                project_qkv(t, 2)

            def output_transposes():
                pe.wait_ge(o_ready, b * TT + TT)
                for j in range(2):
                    pe.wait_ge(pair_free[j], body.pair("ot"))
                    for i in range(2):
                        k = 2 * j + i
                        for t in range(TT):
                            mm = nc.tensor.transpose(pair[j][:, i, t * P:(t + 1) * P], xin[:, t, k * P:(k + 1) * P], ident32[:, :])
                    mm.then_inc(pair_filled[j], 1)

            def output_projection():
                for j in range(2):
                    pe.wait_ge(pair_free[j], body.pair("ot") + 1)
                for t in range(TT):
                    project(("wo", t), lambda p, k: nxb[:, p, k, t * P:(t + 1) * P], lambda q, k: wq[:, 3, q, k, :], KT, bias=3)

            if b is not None:
                output_transposes()
            if f_ is not None:
                qkv(1)
            if b is not None:
                output_projection()
            if f_ is not None:
                qkv(2)
            if b is not None:
                norm_transposes(1, b)
            if f_ is not None:
                qkv(3)
            if b is not None:
                pe.wait_ge(nx_ready[1], b * KT + KT)
                gate_or_up(0, 0)
                gate_or_up(0, 1)
            if f_ is not None:
                stack_transposes(TT - 1)
            if b is not None:
                for f in range(1, FA):
                    gate_or_up(f, 0)
                    gate_or_up(f, 1)
                down(0, 0)
                down(0, 1)
            if n_ is not None and not body.filling:
                norm_transposes(0, n_, range(0, 2))
            if b is not None:
                down(0, 2)
            if n_ is not None and not body.filling:
                norm_transposes(0, n_, range(2, KT))
            if b is not None:
                down(0, 3)
            if f_ is not None:
                pe.wait_ge(pair_free[1], body.pair("max", 0))
            for h in range(H):
                if f_ is not None:
                    scores_by_queries(h)
                    if body.filling and h == FIRST_NORM[3]:
                        norm_transposes(0, n_)
                if b is not None:
                    for n in shared(2 * FB, h):
                        gate_or_up(FA + n // 2, n % 2)
            if b is not None:
                down_steps(range(BEFORE_TURN))
            if f_ is not None:
                pe.wait_ge(nm_ready, f_ + 1)
                n, c = body.turn("mt")
                pe.wait_ge(bank_free[n], c)
                for t in range(TT):
                    mm = nc.tensor.transpose(bank[n][:, :].bitcast(F16)[96:128, t * P:(t + 1) * P],
                                             nm[:, t, :, :].rearrange("p h i -> p (h i)"), ident16[:, :])
                mm.then_inc(bank_filled[n], 1)
            if b is not None:
                down_steps(range(BEFORE_TURN, BEFORE_TURN + AFTER_TURN))
            if f_ is not None:
                pe.wait_ge(mrow_in, f_ * 16 + 16)
            for h in range(H):
                if f_ is not None:
                    scores_by_keys(h)
                if b is not None:
                    if h == 0:
                        down_steps(range(BEFORE_TURN + AFTER_TURN, FB * TT - REST))
                    down_steps(FB * TT - REST + n for n in shared(REST, h))
                if f_ is not None and h:
                    probs_v(h - 1)
            if n_ is not None:
                pe.wait_ge(nx_ready[0], n_ * KT + KT)
                project_qkv(0, 0)
            if f_ is not None:
                probs_v(H - 1)
            if n_ is not None:
                project_qkv(0, 1)
                project_qkv(0, 2)

        bodies(pe, program)

    @block.scalar
    def _(act):
        def program(body):
            n_, f_, b = body.pre, body.front, body.back

            def norm_tiles(i, seq):
                for k in range(KT):
                    ps, filled, free, c = norm_tile(body, i, seq, k)
                    act.wait_ge(filled, c)
                    if k >= 2:
                        act.wait_ge(nx_ready[i], seq * KT + k - 1)
                    elif i == 0 and b is not None:
                        m, d = body.turn("u", FA - 2 + (FA + k) % 2)
                        act.wait_ge(bank_free[m], d + 1)
                    elif i == 0 and f_ is not None:
                        act.wait_ge(nx_ready[i], seq * KT + k - 1)
                    modulation = dict(scale=mods[:, i, 0, k:k + 1], bias=mods[:, i, 1, k:k + 1])
                    nc.scalar.activation(acts[:, k % 2, :], ps, ACT.Identity, **modulation)
                    nc.scalar.activation(nx[i][:, 0, k, :], ps, ACT.Identity, **modulation).then_inc(free, 1)

            def gate(f):
                n, c = body.turn("g", f)
                act.wait_ge(bank_filled[n], c)
                if f < 2:
                    act.wait_ge(nx_ready[1], b * KT + KT - 1 + f)
                elif FA <= f < FA + 2 and n_ is not None:
                    act.wait_ge(nx_ready[0], n_ * KT + KT - 1 + f % 2)
                else:
                    m, d = body.turn("u", f - 2)
                    act.wait_ge(bank_free[m], d + 1)
                nc.scalar.activation(acts[:, f % 2, :], bank[n][:, :], ACT.Gelu, scale=UNSCALE).then_inc(bank_free[n], 1)

            def h_high(f):
                n, c = body.turn("u", f)
                act.wait_ge(bank_free[n], c + 1)
                if f == FA:
                    m, d = body.turn("dn", 0, TT - 1)
                    act.wait_ge(bank_filled[m], d)
                nc.scalar.copy(hT[:, 0, f - FA if f >= FA else f, :], hf[:, f % 2, :]).then_inc(h_hi, 1)

            def q_copy(t):
                act.wait_ge(pair_filled[0], body.pair("st", t))
                nc.scalar.copy(qT[0:96, :, t * P:(t + 1) * P].rearrange("p (g h) s -> p g h s", g=2),
                               pair[0][:, :, :].bitcast(F16)[0:96, :, :].rearrange("p g (h s) -> p g h s", h=8)).then_inc(pair_free[0], 1)

            def take_pv(h):
                act.wait_ge(pv_filled, f_ * H + h + 1)
                nc.scalar.copy(osb[:, :, h, :], pv[:, :, 0:HD])
                nc.scalar.copy(den[:, :, h:h + 1], pv[:, :, 2 * HD:VW]).then_inc(o_copied, 1)

            def qkv(t, seq):
                if t:
                    q_copy(t - 1)
                n, c = body.turn("qkv", t, "v")
                act.wait_ge(bank_filled[n], c)
                nc.scalar.copy(v[:, t, :, 0:HD], bank[n][:, :].rearrange("p (h d) -> p h d", h=H)).then_inc(v_hi, 1)
                for m, name in enumerate("qk"):
                    act.wait_ge(rope_sum, seq * 2 * TT + 2 * t + m + 1)
                    if t:
                        act.wait_ge(pair_filled[m], body.pair("st", t - 1))
                    blocks = stack[:, m, :, :].rearrange("p h (c j) -> p h c j", c=3)
                    dst = blocks[:, :, 0:2, :] if m == 0 else blocks[:, :, 0:3:2, :]
                    src = rt[:, m, 0, :].rearrange("p (h o j) -> p h o j", h=H, o=1).to_broadcast([P, H, 2, HD])
                    nc.scalar.copy(dst, src).then_inc(rope_hi, 1)

            def wo_added(t):
                n, c = body.turn("wo", t)
                act.wait_ge(bank_free[n], c + 1)

            def unit_high(n):
                act.wait_ge(staged[n % 2], 16 * (n // 2 + 1))
                if 2 <= n < N_GU:
                    act.wait_ge(kept[n % 2], 32 * (n // 2))
                (hi, _), src = unit_parts(n)
                nc.scalar.activation(hi, src, ACT.Copy, scale=W_SCALE).then_inc(unit_hi, 1)

            def first_norm():
                act.wait_ge(mods_in[0], n_ * 16 + 16)
                norm_tiles(0, n_)

            if b is not None:
                for j in range(2):
                    act.wait_ge(pair_filled[j], body.pair("ot"))
                    nc.scalar.copy(nxb[:, 0, 2 * j:2 * j + 2, :], pair[j][:, :, :]).then_inc(ot_hi, 1)
            if f_ is not None:
                qkv(1, f_)
                if body.filling:
                    unit_high(UNITS_TOKENS[1])
            if b is not None:
                steps.squares(act, 2, b, x2, wo_added)
                steps.normalise(act, 2, b, x2)
            if f_ is not None:
                qkv(2, f_)
                if body.filling:
                    unit_high(UNITS_TOKENS[2])
            if b is not None:
                act.wait_ge(mods_in[1], b * 16 + 16)
                norm_tiles(1, b)
            if f_ is not None:
                qkv(3, f_)
                if body.filling:
                    unit_high(UNITS_TOKENS[3])
            if b is not None:
                gate(0)
            if f_ is not None:
                q_copy(TT - 1)
            if b is not None:
                for f in range(1, FA):
                    gate(f)
                    h_high(f - 1)
                    if n_ is not None and f == 2:
                        steps.first_squares(act, n_)
                    if n_ is not None and f == 4:
                        steps.second_squares(act, n_)
                h_high(FA - 1)
                if n_ is not None:
                    steps.normalise(act, 1, n_, xin)
            elif body.filling:
                for h in range(H):
                    if h == FIRST_NORM[0]:
                        steps.first_squares(act, n_)
                    if h in UNITS_MAX:
                        unit_high(UNITS_MAX[h])
                    if h == FIRST_NORM[1]:
                        steps.second_squares(act, n_)
                    if h == FIRST_NORM[2]:
                        steps.normalise(act, 1, n_, xin)
                    if h == FIRST_NORM[3]:
                        first_norm()
                for n in UNITS_BETWEEN:
                    unit_high(n)
            if n_ is not None and not body.filling:
                first_norm()
            if body.starting:
                for n in UNITS_AHEAD:
                    unit_high(n)
            if b is not None:
                for f in range(FA, FT):
                    gate(f)
                    if f > FA:
                        h_high(f - 1)
                h_high(FT - 1)
            if f_ is not None:
                for h in range(H):
                    for j in range(2):
                        act.wait_ge(pair_filled[j], body.pair("probs", h))
                        if j == 1:
                            nc.scalar.activation(front[:, h % 2, 0, 2 * S:4 * S].rearrange("p (k s) -> p k s", k=2), pair[j][:, :, :],
                                                 ACT.Exp, scale=INV_SQRT_HD)
                        if h:
                            act.wait_ge(p_ready, f_ * 2 * H + 2 * h + j - 1)
                        nc.scalar.activation(p32[:, j, :].rearrange("p (k s) -> p k s", k=2), pair[j][:, :, :], ACT.Exp,
                                             scale=INV_SQRT_HD).then_inc(pair_free[j], 1)
                    if h:
                        take_pv(h - 1)
                    if body.filling and h in UNITS_PROBS:
                        unit_high(UNITS_PROBS[h])
                take_pv(H - 1)
            if n_ is not None:
                qkv(0, n_)

        bodies(act, program)

    @block.vector
    def _(dve):
        def program(body):
            n_, f_, b = body.pre, body.front, body.back

            def norm_split(i, seq, tiles=range(KT)):
                for k in tiles:
                    _, _, free, c = norm_tile(body, i, seq, k)
                    dve.wait_ge(free, c + 1)
                    nc.vector.tensor_tensor(nx[i][:, 1, k, :], acts[:, k % 2, :], nx[i][:, 0, k, :], ALU.subtract).then_inc(nx_ready[i], 1)

            def gate_by_up(f):
                n, c = body.turn("u", f)
                m, d = body.turn("g", f)
                dve.wait_ge(bank_free[m], d + 1)
                dve.wait_ge(bank_filled[n], c)
                if f >= 2:
                    dve.wait_ge(h_ready, b * FT + f - 1)
                nc.vector.tensor_tensor(hf[:, f % 2, :], bank[n][:, :], acts[:, f % 2, :], ALU.mult).then_inc(bank_free[n], 1)

            def h_low(f):
                dve.wait_ge(h_hi, b * FT + f + 1)
                slot = f - FA if f >= FA else f
                nc.vector.tensor_tensor(hT[:, 1, slot, :], hf[:, f % 2, :], hT[:, 0, slot, :], ALU.subtract).then_inc(h_ready, 1)

            def add(step, t):
                n, c = body.turn(*step)
                dve.wait_ge(bank_filled[n], c)
                nc.vector.scalar_tensor_tensor(out=x2[:, t, :], in0=bank[n][:, :], scalar=UNSCALE * UNSCALE, in1=x2[:, t, :],
                                               op0=ALU.mult, op1=ALU.add).then_inc(bank_free[n], 1)

            def k_copy(t):
                dve.wait_ge(pair_filled[1], body.pair("st", t))
                nc.vector.tensor_copy(kT[0:96, :, t * P:(t + 1) * P].rearrange("p (g h) s -> p g h s", g=2),
                                      pair[1][:, :, :].bitcast(F16)[0:96, :, :].rearrange("p g (h s) -> p g h s", h=8)).then_inc(pair_free[1], 1)

            def rotate(t, seq, m):
                n, c = body.turn("qkv", t, "qk"[m])
                dve.wait_ge(bank_filled[n], c)
                q = bank[n][:, :].rearrange("p (h c j) -> p h c j", h=H, c=2)
                r = rt[:, m, :, :].rearrange("p i (h c j) -> p i h c j", h=H, c=2)
                tab = rope[:, t, :, :].rearrange("p a (o c j) -> p a o c j", o=1, c=2)
                if t:
                    dve.wait_ge(rope_ready, seq * 2 * TT + 2 * (t - 1) + m + 1)
                nc.vector.tensor_tensor(rt[:, m, 0, :].rearrange("p (h j) -> p h j", h=H), bank[n][:, :].rearrange("p (h j) -> p h j", h=H),
                                        rope[:, t, 0:1, :].to_broadcast([P, H, HD]), ALU.mult)
                for a in range(2):
                    ins = nc.vector.tensor_tensor(r[:, 1, :, a, :], q[:, :, 1 - a, :],
                                                  tab[:, 1, :, a, :].to_broadcast([P, H, HD // 2]), ALU.mult)
                ins.then_inc(bank_free[n], 1)
                dve.wait_ge(bank_free[n], c + 1)
                nc.vector.tensor_tensor(rt[:, m, 0, :], rt[:, m, 0, :], rt[:, m, 1, :], ALU.add).then_inc(rope_sum, 1)

            def rope_tile(t, seq, rotations=range(2)):
                for m in rotations:
                    rotate(t, seq, m)
                if t:
                    k_copy(t - 1)
                n, c = body.turn("qkv", t, "v")
                dve.wait_ge(v_hi, seq * TT + t + 1)
                nc.vector.tensor_tensor(v[:, t, :, HD:2 * HD], bank[n][:, :].rearrange("p (h d) -> p h d", h=H),
                                        v[:, t, :, 0:HD], ALU.subtract).then_inc(bank_free[n], 1)
                for m in range(2):
                    dve.wait_ge(rope_hi, seq * 2 * TT + 2 * t + m + 1)
                    lo = 2 * HD if m == 0 else HD
                    nc.vector.tensor_tensor(stack[:, m, :, lo:lo + HD], rt[:, m, 0, :].rearrange("p (h j) -> p h j", h=H),
                                            stack[:, m, :, 0:HD], ALU.subtract).then_inc(rope_ready, 1)

            def unit_low(n):
                dve.wait_ge(unit_hi, n + 1)
                (hi, lo), src = unit_parts(n)
                nc.vector.scalar_tensor_tensor(out=lo, in0=src, scalar=W_SCALE, in1=hi, op0=ALU.mult, op1=ALU.subtract).then_inc(unit_lo, 1)

            def head_max(h):
                for j in range(2):
                    dve.wait_ge(pair_filled[j], body.pair("max", h))
                    nc.vector.tensor_reduce(mx[:, h, 2 * j:2 * j + 2], pair[j][:, :, :], AX_X, ALU.max).then_inc(pair_free[j], 1)

            def negated_maxima():
                for j in range(2):
                    dve.wait_ge(pair_free[j], body.pair("max", H - 1) + 1)
                nc.vector.tensor_scalar(nmf[:, :, :], mx[:, :, :].rearrange("p h t -> p t h"), -1.0, LN_SCALE * float(HD) ** 0.5,
                                        ALU.mult, ALU.add).then_inc(nm_step, 1)
                dve.wait_ge(nm_step, f_ * 2 + 1)
                nc.vector.tensor_copy(nm[:, :, :, 0], nmf[:, :, :]).then_inc(nm_step, 1)
                dve.wait_ge(nm_step, f_ * 2 + 2)
                nc.vector.tensor_tensor(nm[:, :, :, 1], nmf[:, :, :], nm[:, :, :, 0], ALU.subtract).then_inc(nm_ready, 1)

            def split_probs(h):
                for j in range(2):
                    if j == 0 and h >= 2:
                        dve.wait_ge(pv_filled, f_ * H + h - 1)
                    dve.wait_ge(pair_free[j], body.pair("probs", h) + 1)
                    hi = front[:, h % 2, 0, j * 2 * S:(j + 1) * 2 * S]
                    lo = front[:, h % 2, 1, j * 2 * S:(j + 1) * 2 * S]
                    if j == 0:
                        nc.vector.tensor_copy(hi, p32[:, j, :]).then_inc(p_hi, 1)
                        dve.wait_ge(p_hi, f_ * H + h + 1)
                    nc.vector.tensor_tensor(lo, p32[:, j, :], hi, ALU.subtract).then_inc(p_ready, 1)

            def add_pv(h):
                dve.wait_ge(o_copied, f_ * H + h + 1)
                nc.vector.tensor_tensor(osb[:, :, h, :], osb[:, :, h, :], pv[:, :, HD:2 * HD], ALU.add).then_inc(pv_free, 1)

            if b is not None:
                for j in range(2):
                    dve.wait_ge(ot_hi, b * 2 + j + 1)
                    nc.vector.tensor_tensor(nxb[:, 1, 2 * j:2 * j + 2, :], pair[j][:, :, :], nxb[:, 0, 2 * j:2 * j + 2, :],
                                            ALU.subtract).then_inc(pair_free[j], 1)
            if f_ is not None:
                rope_tile(1, f_)
                if body.filling:
                    unit_low(UNITS_TOKENS[1])
            if b is not None:
                dve.wait_ge(x1_in, b * 16 + 16)
                for t in range(TT):
                    add(("wo", t), t)
            if f_ is not None:
                rope_tile(2, f_)
                if body.filling:
                    unit_low(UNITS_TOKENS[2])
            if b is not None:
                norm_split(1, b)
            if f_ is not None:
                rope_tile(3, f_)
                if body.filling:
                    unit_low(UNITS_TOKENS[3])
            if b is not None:
                gate_by_up(0)
            if f_ is not None:
                k_copy(TT - 1)
            if b is not None:
                for f in range(1, FA):
                    gate_by_up(f)
                    h_low(f - 1)
                    if n_ is not None and f == 3:
                        steps.modulate(dve, n_, 0)
                        steps.modulate(dve, n_, 1)
                h_low(FA - 1)
                add(("dn", 0, 0), 0)
                add(("dn", 0, 1), 1)
            if n_ is not None and not body.filling:
                norm_split(0, n_, range(0, 2))
            if b is not None:
                add(("dn", 0, 2), 2)
            if n_ is not None and not body.filling:
                norm_split(0, n_, range(2, KT))
            if body.starting:
                for n in UNITS_AHEAD:
                    unit_low(n)
            if b is not None:
                add(("dn", 0, 3), 3)
            for h in range(H + 1):
                if f_ is not None and h < H:
                    head_max(h)
                    if body.filling:
                        if h == FIRST_NORM[0]:
                            steps.modulate(dve, n_, 0)
                        if h == FIRST_NORM[1]:
                            steps.modulate(dve, n_, 1)
                        if h == FIRST_NORM[3]:
                            norm_split(0, n_)
                        if h in UNITS_MAX:
                            unit_low(UNITS_MAX[h])
                if b is not None:
                    for f in range(FA, FT):
                        if last_head(2 * (f - FA) + 1, 2 * FB) == h - 1:
                            gate_by_up(f)
                            if f > FA:
                                h_low(f - 1)
            if b is not None:
                h_low(FT - 1)
            if f_ is not None:
                negated_maxima()
            if f_ is not None:
                n, c = body.turn("mt")
                dve.wait_ge(bank_filled[n], c)
                nc.vector.tensor_copy(mrow[96:128, :], bank[n][:, :].bitcast(F16)[96:128, 0:S]).then_inc(bank_free[n], 1)
            if body.filling:
                for n in UNITS_BETWEEN:
                    unit_low(n)
            if b is not None:
                add(("dn", 1, 0), 0)
            for h in range(H + 1):
                if f_ is not None and h < H:
                    split_probs(h)
                    if h:
                        add_pv(h - 1)
                    if body.filling and h in UNITS_PROBS:
                        unit_low(UNITS_PROBS[h])
                if b is not None:
                    for t in range(1, TT):
                        if last_head(FB * (t + 1) - 1 - (FB * TT - REST), REST) == h - 1:
                            add(("dn", 1, t), t)
            if n_ is not None:
                rotate(0, n_, 0)
            if f_ is not None:
                add_pv(H - 1)
                nc.vector.reciprocal(rden[:, :, :], den[:, :, :]).then_inc(rden_ready, 1)
                dve.wait_ge(rden_ready, f_ + 1)
                dve.wait_ge(pv_free, f_ * H + H + 1)
                for t in range(TT):
                    nc.vector.tensor_tensor(osb[:, t, :, :], osb[:, t, :, :],
                                            rden[:, t, :].rearrange("p (h o) -> p h o", o=1).to_broadcast([P, H, HD]), ALU.mult).then_inc(o_ready, 1)
            if n_ is not None:
                rope_tile(0, n_, rotations=[1])

        bodies(dve, program)


def block_kernel(nc, w, out):
    with ExitStack() as ctx:
        def sb(name, shape, dt):
            return ctx.enter_context(nc.sbuf_tensor(name, shape, dt))

        def sem(name):
            return ctx.enter_context(nc.semaphore(name))

        res = {
            "wqkvo": sb("wqkvo", [P, 4, 2, KT, 512], F16),
            "wdn": sb("wdn", [P, 2, FT, 512], F16),
            "ident16": sb("ident16", [P, P], F16),
            "ident32": sb("ident32", [P, P], F32),
            "rope": sb("rope", [P, TT, 2, HD], F32),
            "kT": sb("kT", [P, H, S], F16),
            "v": sb("v", [P, TT, H, VW], F16),
            "brow": sb("brow", [P, 512], F16),
            "bones": sb("bones", [P, 4, P], F16),
            "bank_free": [sem(f"bank{k}_free") for k in range(RING)],
            "pair_free": [sem(f"pair{j}_free") for j in range(2)],
            "pv_free": sem("pv_free"), "stored": sem("stored"),
        }
        res["residual"] = Residual(nc, sb, sem)
        res["free"] = [*res["bank_free"], *res["pair_free"], res["pv_free"], res["stored"]]
        scratch = {
            "gu": nc.dram_tensor("gu_split", (FT, P, 2, 2, KT, P), F16).ap(),
            "x1": nc.dram_tensor("x1_saved_dram", (B, P, TT, D), F32).ap(),
            "rows": nc.dram_tensor("rows_all", (B, 1024), F32).ap(),
            "mods": nc.dram_tensor("mods_all", (B, P, 4 * KT), F32).ap(),
        }
        with ExitStack() as inner:
            prepare(nc, inner, w, res, scratch)
        with ExitStack() as inner:
            sequences(nc, inner, w, res, scratch, out)


_INS = {
    "x": "x", "cond_1024": "cond", "L0_cond_w_proj": "w_proj", "L0_cond_b_proj": "b_proj", "L0_cond_rms_weight": "rms_weight",
    "L1_cond_t1_w1": "t1_w1", "L1_cond_t1_w2": "t1_w2", "L1_cond_t2_w1": "t2_w1", "L1_cond_t2_w2": "t2_w2",
    "L1_cond_wq": "wq", "L1_cond_bq": "bq", "L1_cond_wk": "wk", "L1_cond_bk": "bk", "L1_cond_wv": "wv", "L1_cond_bv": "bv",
    "L1_cond_wo": "wo", "L1_cond_bo": "bo", "L1_cond_w_gate": "w_gate", "L1_cond_w_up": "w_up", "L1_cond_w_down": "w_down",
}


def _constants():
    import numpy as np
    freq = (np.float32(1.0) / np.float32(10000.0) ** (np.arange(0, 32, 2, dtype=np.float32) / np.float32(32))).astype(np.float32)
    angle = np.arange(512, dtype=np.float32)[:, None] * freq[None, :]
    c, s = np.cos(angle), np.sin(angle)
    rope = np.stack([np.concatenate([c, c], 1), np.concatenate([-s, s], 1)], 1).astype(np.float32) / np.float32(256)
    pick = (np.arange(32)[:, None] // 2 == np.arange(16)[None, :]).astype(np.float16)
    bones = np.zeros((128, 4, 128), np.float16)
    for m in range(4):
        bones[[m, 4 + m], m, :] = 1 if m < 3 else 256
    return {"bones": bones, "ident16": np.eye(128, dtype=np.float16), "ident32": np.eye(128, dtype=np.float32), "rope": rope, "pick": pick}


def _by_features(inputs):
    import numpy as np
    cols = lambda name: np.asarray(inputs["L1_cond_" + name]).reshape(-1, 128).T
    vecs = [np.concatenate([cols(f"t{i}_b1"), cols(f"t{i}_b2"), cols(f"w_norm{i}")], 1) for i in (1, 2)]
    cond_t = np.asarray(inputs["cond_1024"]).T.reshape(4, 128, 8).transpose(1, 0, 2)
    return {"vecs": np.stack(vecs, 1), "cond_t": cond_t}


def kernel(**inputs):
    import numpy as _np
    import concourse.bacc as _bacc
    from concourse import mybir as _mybir
    from concourse.bass_utils import run_bass_kernel_spmd as _run

    nc = _bacc.Bacc("TRN2", target_bir_lowering=False, num_devices=1)
    arrays, aps = {}, {}
    named = [(_INS[k], inputs[k]) for k in _INS] + list(_constants().items()) + list(_by_features(inputs).items())
    for name, value in named:
        a = _np.ascontiguousarray(value)
        arrays[f"in_{name}_dram"] = a
        aps[name] = nc.dram_tensor(f"in_{name}_dram", a.shape, _mybir.dt.from_np(a.dtype), kind="ExternalInput").ap()
    out = nc.dram_tensor("out_0_dram", (8, 512, 512), _mybir.dt.float32, kind="ExternalOutput").ap()
    block_kernel(nc, aps, out)
    r = _run(nc, [arrays], core_ids=[0])
    return r.results[0]["out_0_dram"]
```
